# Optimizing a Trainium2 kernel written in Bass

```python
import numpy as np
import jax
import jax.numpy as jnp

def _softmax(x, axis=-1):
    return jax.nn.softmax(x, axis=axis)

def _gelu(x):
    return jax.nn.gelu(x, approximate=True)

def _silu(x):
    return jax.nn.silu(x)

def _sigmoid(x):
    return jax.nn.sigmoid(x)

def _layernorm(x, axis=-1, eps=1e-05):
    m = jnp.mean(x, axis=axis, keepdims=True)
    v = jnp.var(x, axis=axis, keepdims=True)
    return (x - m) / jnp.sqrt(v + eps)

def _scatter_add(tgt, idx, src, axis=0):
    return tgt.at[idx].add(src)

def _segment_sum(src, seg, n):
    return jax.ops.segment_sum(src, seg, n)
kernel_name = 'mk_seq_postln_d1_jaxref_r8_93a8d7'

def setup_inputs(seed: int=0):
    np.random.seed(seed)
    _w = jnp.asarray

    def _L0_attn_setup():
        import jax, jax.numpy as jnp
        import numpy as np
        H = 32
        G = 8
        D = 128
        HID = 512
        THETA = 10000.0

        def _rope(x, pos):
            half = D // 2
            inv_freq = 1.0 / THETA ** (jnp.arange(0, half, dtype=jnp.float32) / half)
            ang = pos[:, None].astype(jnp.float32) * inv_freq[None, :]
            cos = jnp.cos(ang)[None, None]
            sin = jnp.sin(ang)[None, None]
            x1, x2 = (x[..., :half], x[..., half:])
            return jnp.concatenate([x1 * cos - x2 * sin, x1 * sin + x2 * cos], axis=-1)
        key = jax.random.key(seed)
        ks = jax.random.split(key, 9)
        s = 0.02
        return {'hidden_states': jax.random.normal(ks[0], (1, 256, HID), jnp.float32), 'Wq': jax.random.normal(ks[1], (HID, H * D), jnp.float32) * s, 'bq': jnp.zeros((H * D,), jnp.float32), 'Wk': jax.random.normal(ks[2], (HID, G * D), jnp.float32) * s, 'bk': jnp.zeros((G * D,), jnp.float32), 'Wv': jax.random.normal(ks[3], (HID, G * D), jnp.float32) * s, 'bv': jnp.zeros((G * D,), jnp.float32), 'Wo': jax.random.normal(ks[4], (H * D, HID), jnp.float32) * s, 'bo': jnp.zeros((HID,), jnp.float32)}
    _L0_attn_in = _L0_attn_setup()

    def _L0_ffn_setup():
        import jax, jax.numpy as jnp
        import numpy as np
        SCALING = 16.0 / 8.0
        GAMMA = 1.0
        EPS = 1e-12
        key = jax.random.key(seed)
        ks = jax.random.split(key, 8)
        B, T, H, O = (4, 256, 512, 512)
        E_tot, E_act, r = (16, 4, 8)
        return {'x': jax.random.normal(ks[0], (B, T, H), jnp.float32), 'W_base': jax.random.normal(ks[1], (O, H), jnp.float32) * 0.02, 'b_base': jax.random.normal(ks[2], (O,), jnp.float32) * 0.02, 'lora_A': jax.random.normal(ks[3], (E_tot, r, H), jnp.float32) * 0.02, 'lora_B': jax.random.normal(ks[4], (E_tot, O, r), jnp.float32) * 0.02, 'router_W': jax.random.normal(ks[5], (E_tot, H), jnp.float32) * 0.02, 'router_b': jax.random.normal(ks[6], (E_tot,), jnp.float32) * 0.02, 'domain_prior': jax.random.uniform(ks[7], (E_tot,), jnp.float32), 'active': jnp.arange(E_act, dtype=jnp.int32)}
    _L0_ffn_in = _L0_ffn_setup()
    _d = {'L0_attn_hidden_states': _L0_attn_in['hidden_states'], 'L0_attn_Wq': _L0_attn_in['Wq'], 'L0_attn_bq': _L0_attn_in['bq'], 'L0_attn_Wk': _L0_attn_in['Wk'], 'L0_attn_bk': _L0_attn_in['bk'], 'L0_attn_Wv': _L0_attn_in['Wv'], 'L0_attn_bv': _L0_attn_in['bv'], 'L0_attn_Wo': _L0_attn_in['Wo'], 'L0_attn_bo': _L0_attn_in['bo'], 'L0_ffn_W_base': _L0_ffn_in['W_base'], 'L0_ffn_b_base': _L0_ffn_in['b_base'], 'L0_ffn_lora_A': _L0_ffn_in['lora_A'], 'L0_ffn_lora_B': _L0_ffn_in['lora_B'], 'L0_ffn_router_W': _L0_ffn_in['router_W'], 'L0_ffn_router_b': _L0_ffn_in['router_b'], 'L0_ffn_domain_prior': _L0_ffn_in['domain_prior'], 'L0_ffn_active': _L0_ffn_in['active']}
    _x0 = _d['L0_attn_hidden_states']
    _d['L0_attn_hidden_states'] = jax.random.normal(jax.random.fold_in(jax.random.key(seed), 1), (2, 512, 512), dtype=_x0.dtype)
    del _x0
    return _d

def reference(L0_attn_hidden_states, L0_attn_Wq, L0_attn_bq, L0_attn_Wk, L0_attn_bk, L0_attn_Wv, L0_attn_bv, L0_attn_Wo, L0_attn_bo, L0_ffn_W_base, L0_ffn_b_base, L0_ffn_lora_A, L0_ffn_lora_B, L0_ffn_router_W, L0_ffn_router_b, L0_ffn_domain_prior, L0_ffn_active):

    def _L0_attn_ref(hidden_states, Wq, bq, Wk, bk, Wv, bv, Wo, bo):
        import jax, jax.numpy as jnp
        import numpy as np
        H = 32
        G = 8
        D = 128
        HID = 512
        THETA = 10000.0

        def _rope(x, pos):
            half = D // 2
            inv_freq = 1.0 / THETA ** (jnp.arange(0, half, dtype=jnp.float32) / half)
            ang = pos[:, None].astype(jnp.float32) * inv_freq[None, :]
            cos = jnp.cos(ang)[None, None]
            sin = jnp.sin(ang)[None, None]
            x1, x2 = (x[..., :half], x[..., half:])
            return jnp.concatenate([x1 * cos - x2 * sin, x1 * sin + x2 * cos], axis=-1)
        B, S, _ = hidden_states.shape
        R = H // G
        q = hidden_states @ Wq + bq
        k = hidden_states @ Wk + bk
        v = hidden_states @ Wv + bv
        q = q.reshape(B, S, H, D).transpose(0, 2, 1, 3)
        k = k.reshape(B, S, G, D).transpose(0, 2, 1, 3)
        v = v.reshape(B, S, G, D).transpose(0, 2, 1, 3)
        pos = jnp.arange(S)
        q = _rope(q, pos)
        k = _rope(k, pos)
        qg = q.reshape(B, G, R, S, D)
        scores = jnp.einsum('bgrsd,bgtd->bgrst', qg, k) / jnp.sqrt(jnp.float32(D))
        causal = jnp.tril(jnp.ones((S, S), dtype=bool))
        scores = jnp.where(causal[None, None, None], scores, jnp.finfo(scores.dtype).min)
        probs = jax.nn.softmax(scores, axis=-1)
        ctx = jnp.einsum('bgrst,bgtd->bgrsd', probs, v)
        ctx = ctx.reshape(B, H, S, D).transpose(0, 2, 1, 3).reshape(B, S, H * D)
        return ctx @ Wo + bo

    def _L0_ffn_ref(x, W_base, b_base, lora_A, lora_B, router_W, router_b, domain_prior, active):
        import jax, jax.numpy as jnp
        import numpy as np
        SCALING = 16.0 / 8.0
        GAMMA = 1.0
        EPS = 1e-12
        y = jnp.einsum('bth,oh->bto', x, W_base) + b_base
        A = lora_A[active]
        Bm = lora_B[active]
        z = jnp.einsum('bth,erh->bter', x, A)
        contribs = jnp.einsum('bter,eor->bteo', z, Bm) * SCALING
        logits = jnp.einsum('bth,eh->bte', x, router_W) + router_b
        logits = logits[..., active]
        prior = domain_prior[active]
        alpha = jax.nn.softmax(jnp.log(prior + EPS) + logits / GAMMA, axis=-1)
        return y + jnp.einsum('bteo,bte->bto', contribs, alpha)
    x = L0_attn_hidden_states
    x = _layernorm(x + _L0_attn_ref(x, L0_attn_Wq, L0_attn_bq, L0_attn_Wk, L0_attn_bk, L0_attn_Wv, L0_attn_bv, L0_attn_Wo, L0_attn_bo), axis=-1)
    x = _layernorm(x + _L0_ffn_ref(x, L0_ffn_W_base, L0_ffn_b_base, L0_ffn_lora_A, L0_ffn_lora_B, L0_ffn_router_W, L0_ffn_router_b, L0_ffn_domain_prior, L0_ffn_active), axis=-1)
    return x

_drawn_inputs = setup_inputs


def setup_inputs(seed=0):
    import zlib

    import numpy as np

    out = dict(_drawn_inputs(seed))
    spreads = {'L0_attn_bq': (0.0, 0.8),
     'L0_attn_bk': (0.0, 0.8),
     'L0_attn_bv': (0.0, 0.1),
     'L0_attn_bo': (0.0, 0.1)}
    factors = {'L0_attn_Wq': 4.724,
     'L0_attn_Wk': 4.62,
     'L0_ffn_b_base': 3.238,
     'L0_ffn_router_W': 6.693,
     'L0_ffn_router_b': 200.0,
     'L0_ffn_domain_prior': 200.0}
    for name, (base, spread) in spreads.items():
        noise = np.random.default_rng([zlib.crc32(name.encode()), seed]).standard_normal(out[name].shape)
        drawn = base * np.exp(spread * noise) if base else spread * noise
        out[name] = jnp.asarray(drawn.astype(out[name].dtype))
    for name, factor in factors.items():
        out[name] = (out[name] * factor).astype(out[name].dtype)
    return out
```

```python
import concourse.bass as bass
from concourse import mybir
from contextlib import ExitStack

F32 = mybir.dt.float32
F32R = mybir.dt.float32r
I32 = mybir.dt.int32
ALU = mybir.AluOpType
ACT = mybir.ActivationFunctionType

P = 128
B, S, HID = 2, 512, 512
H, G, D = 32, 8, 128
R = H // G
KT = HID // P
TT = S // P
NT = B * TT
STEPS = B * R
E, RANK = 16, 8
ER = E * RANK
ARW = 256
SCALE = float(D) ** -0.5
LORA_SCALING = 16.0 / 8.0
LN_EPS = 1e-05
PRIOR_EPS = 1e-12
BIG = 3.0e38
OFF = -1.0e37

SCOL = [0, 128, 384, 768, 1280]
PT_ZERO, PT_T3, PT_T1, PT_T0, PT_T2, PT_END = 0, 128, 256, 640, 1152, 1408

PROJ_Q = [0, 2, 3, 5, 6, 8, 9, 11]
PROJ_KV = {0: 1, 2: 4, 4: 7, 6: 10}
PROJ_PER = 12
ROPES_UP_TO = [1, 2, 3, 4, 4, 5, 6, 7, 8, 9, 9, 10]
ROPE_Q = [0, 2, 3, 4, 5, 7, 8, 9]
ROPE_K = {0: 1, 4: 6}
ROPE_PER = 10
TR_P = [0, 3, 6, 9, 13, 16, 19, 22]
TR_V = {3: 12, 7: 25}
TR_PER = 26
TR_X = NT
SC_PER = 3
TR_TAIL = TR_X + 1 + TR_PER * (G - 1) + 25
N_PREP = 7


def kv_shift(g, n):
    return 1 if isinstance(g, int) and g < 0 and n == 4 else 0


def q_shift(g, n):
    return -1 if isinstance(g, int) and g == G - 1 and n == 5 else 0


def proj_q(g, n):
    return 4 + PROJ_PER * g + PROJ_Q[n] + q_shift(g, n)


def bank_q(g, n):
    return (PROJ_Q[n] + q_shift(g, n)) % 2


def bank_kv(g, n):
    return (PROJ_KV[n] + kv_shift(g, n)) % 2


def ropes_before(g, j):
    return 3 + ROPE_PER * g + (ROPES_UP_TO[j - 2] if j >= 2 else ROPES_UP_TO[j - 2] - ROPE_PER)


def proj_kv(g, n):
    return 4 + PROJ_PER * g + PROJ_KV[n] + kv_shift(g, n)


def rope_q(g, n):
    return 3 + ROPE_PER * g + ROPE_Q[n] + q_shift(g, n)


def rope_k(g, n):
    return 3 + ROPE_PER * g + ROPE_K[n] + kv_shift(g, n)


def rope_slot(j):
    return (3 + j) % 2


def tr_no(g, j):
    return TR_X + 1 + TR_PER * g + j


def layer_program(nc, x, wq, bq, wk, bk, wv, bv, wo, bo, w_base, b_base, lora_a, lora_b,
                  router_w, router_b, prior, active, cos_t, sin_t, ident_t, mask_t, ids_t, out):
    x_v = x.rearrange("b (t p) h -> p (b t) h", p=P)
    out_v = out.rearrange("b (t p) h -> p (b t) h", p=P)
    wq_v = wq.rearrange("(k p) n -> p k n", p=P)
    wk_v = wk.rearrange("(k p) n -> p k n", p=P)
    wv_v = wv.rearrange("(k p) n -> p k n", p=P)
    wo_v = wo.rearrange("(h d) n -> d h n", d=D)

    ctx = ExitStack()
    with ctx:
        def sb(name, shape, dt=F32):
            return ctx.enter_context(nc.sbuf_tensor(name, shape, dt))

        def ps(name):
            return ctx.enter_context(nc.psum_tensor(name, [P, 512], F32))

        def sem(name):
            return ctx.enter_context(nc.semaphore(name))

        xT_hi = sb("xT_hi", [P, KT, B * S], F32R)
        xT_lo = sb("xT_lo", [P, KT, B * S], F32R)
        acc = sb("acc", [P, NT, HID])
        wq_raw = sb("wq_raw", [P, KT, R * D])
        wk_raw = sb("wk_raw", [P, KT, D])
        wv_raw = sb("wv_raw", [P, KT, D])
        wo_raw = sb("wo_raw", [P, R, HID])
        wq_hi = sb("wq_hi", [P, R, KT, D], F32R)
        wq_lo = sb("wq_lo", [P, R, KT, D], F32R)
        wkv_hi = sb("wkv_hi", [P, 2, KT, D], F32R)
        wkv_lo = sb("wkv_lo", [P, 2, KT, D], F32R)
        wo_hi = sb("wo_hi", [P, R, HID], F32R)
        wo_lo = sb("wo_lo", [P, R, HID], F32R)
        k_hi = sb("k_hi", [P, B, S], F32R)
        k_lo = sb("k_lo", [P, B, S], F32R)
        v_hi = sb("v_hi", [P, B, TT, D], F32R)
        v_lo = sb("v_lo", [P, B, TT, D], F32R)
        q_hi = sb("q_hi", [P, 2, S], F32R)
        q_lo = sb("q_lo", [P, 2, S], F32R)
        rope_cos = sb("rope_cos", [P, 2, S])
        rope_rot = sb("rope_rot", [P, 2, S])
        vT = sb("vT", [P, S])
        prob = sb("prob", [P, 2, SCOL[4]])
        pT_hi = sb("pT_hi", [P, PT_END], F32R)
        pT_lo = sb("pT_lo", [P, PT_END], F32R)
        ctx_hi = sb("ctx_hi", [P, B, R, S], F32R)
        ctx_lo = sb("ctx_lo", [P, B, R, S], F32R)
        cos_sb = sb("cos_sb", [P, S])
        sin_sb = sb("sin_sb", [P, S])
        mask_sb = sb("mask_sb", [P, S])
        ident = sb("ident", [P, P])
        bias_rows = sb("bias_rows", [H + 2 * G, D])
        bias_cols = sb("bias_cols", [P, H + 2 * G])
        row_bias = sb("row_bias", [P, HID])
        negmax = sb("negmax", [P, 2, TT])
        rowsum = sb("rowsum", [P, 2, TT])
        rinv = sb("rinv", [P, 2, TT])
        rt_raw = sb("rt_raw", [E, HID])
        ids_sb = sb("ids_sb", [P, E])
        act_i = sb("act_i", [P, 4], I32)
        act_f = sb("act_f", [P, 4])
        cnt = sb("cnt", [P, 5, E])
        prior_sb = sb("prior_sb", [P, E])
        rb_sb = sb("rb_sb", [P, E])
        logit_c = sb("logit_c", [P, 4, E])
        neg_half = sb("neg_half", [P, 1])
        lnst = sb("lnst", [P, 2, 16])
        sm = sb("sm", [P, 2, 4, E])
        sms = sb("sms", [P, 2, 4])
        wb_raw, la_raw, lb_raw = wq_raw, wk_raw, wv_raw
        wbT_hi = wq_hi[:].rearrange("p r k d -> p r (k d)")
        wbT_lo = wq_lo[:].rearrange("p r k d -> p r (k d)")
        ar_hi = wkv_hi[:].rearrange("p a k d -> p (a k d)").rearrange("p (k c) -> p k c", c=ARW)
        ar_lo = wkv_lo[:].rearrange("p a k d -> p (a k d)").rearrange("p (k c) -> p k c", c=ARW)
        lbT_hi, lbT_lo = k_hi[:, 0, :], k_lo[:, 0, :]
        lb_jer = vT
        zz = rope_rot[:, :, 0:ER]
        zT_hi, zT_lo = q_hi[:, :, 0:P], q_lo[:, :, 0:P]

        ps_proj = [ps("ps_proj0"), ps("ps_proj1")]
        ps_sc = [ps("ps_sc0"), ps("ps_sc1")]
        ps_tr = [ps("ps_tr0"), ps("ps_tr1")]
        ps_ctx = ps("ps_ctx")
        ps_out = ps("ps_out")

        x_in = [sem("x_in0"), sem("x_in1")]
        ident_in, bias_in, rope_in, mask_in = sem("ident_in"), sem("bias_in"), sem("rope_in"), sem("mask_in")
        bo_in, small_in = sem("bo_in"), sem("small_in")
        wq_in, wk_in, wv_in, wo_in = sem("wq_in"), sem("wk_in"), sem("wv_in"), sem("wo_in")
        wb_in, la_in, lb_in, rt_in, bb_in = sem("wb_in"), sem("la_in"), sem("lb_in"), sem("rt_in"), sem("bb_in")
        out_done = sem("out_done")
        bias_tr, bias_done, acc_init = sem("bias_tr"), sem("bias_done"), sem("acc_init")
        zero_done, const_done = sem("zero_done"), sem("const_done")
        wq_hi_d, wq_lo_d = sem("wq_hi_d"), sem("wq_lo_d")
        wk_hi_d, wk_lo_d = sem("wk_hi_d"), sem("wk_lo_d")
        wv_hi_d, wv_lo_d = sem("wv_hi_d"), sem("wv_lo_d")
        wo_hi_d, wo_lo_d = sem("wo_hi_d"), sem("wo_lo_d")
        proj_done, evac_done = sem("proj_done"), sem("evac_done")
        cos_done, sin_done, rope_done = sem("cos_done"), sem("sin_done"), sem("rope_done")
        qk_hi_d, qk_lo_d = sem("qk_hi_d"), sem("qk_lo_d")
        sc_done, max_done, exp_done = sem("sc_done"), sem("max_done"), sem("exp_done")
        rinv_done, p_ready = sem("rinv_done"), sem("p_ready")
        tr_done, tr_hi_d, tr_lo_d = sem("tr_done"), sem("tr_hi_d"), sem("tr_lo_d")
        pv_done, ctx_hi_d, ctx_lo_d = sem("pv_done"), sem("ctx_hi_d"), sem("ctx_lo_d")
        wo_done, acc_done = sem("wo_done"), sem("acc_done")
        dve_chain, ln_done = sem("dve_chain"), sem("ln_done")
        ve_done, rstd_done, x1b_done = sem("ve_done"), sem("rstd_done"), sem("x1b_done")
        lb_sorted, pad_done, ln_prior, prior_eps = sem("lb_sorted"), sem("pad_done"), sem("ln_prior"), sem("prior_eps")
        z_done, nmx_done, e_done, zz_done = sem("z_done"), sem("nmx_done"), sem("e_done"), sem("zz_done")
        y_done, h2_done = sem("y_done"), sem("h2_done")

        def wait(eng, s, value):
            if isinstance(value, int) and value <= 0:
                return
            eng.wait_ge(s, value)

        def has(g):
            if not isinstance(g, int):
                return True, True, True
            return 1 <= g <= G, 0 <= g < G, g < G - 1

        def three(out_ap, w_hi, w_lo, m_hi, m_lo, first, last):
            nc.tensor.matmul(out_ap, w_hi, m_hi, start=first, stop=False)
            nc.tensor.matmul(out_ap, w_hi, m_lo, start=False, stop=False)
            return nc.tensor.matmul(out_ap, w_lo, m_hi, start=False, stop=last)

        block = ctx.enter_context(nc.Block())

        @block.sync
        def _(sp):
            for b in range(B):
                sp.dma_start(acc[:, b * TT:(b + 1) * TT, :], x_v[:, b * TT:(b + 1) * TT, :]).then_inc(x_in[b], 16)
                if b == 0:
                    sp.dma_start(wk_raw[:], wk_v[:, :, 0:D]).then_inc(wk_in, 16)
                    sp.dma_start(wq_raw[:], wq_v[:, :, 0:R * D]).then_inc(wq_in, 16)
                    sp.dma_start(wv_raw[:], wv_v[:, :, 0:D]).then_inc(wv_in, 16)
            sp.dma_start(mask_sb[:], mask_t).then_inc(mask_in, 16)
            sp.dma_start(wo_raw[:], wo_v[:, 0:R, :]).then_inc(wo_in, 16)
            with sp.Fori(1, G) as g:
                sp.wait_ge(wk_lo_d, g)
                sp.dma_start(wk_raw[:], wk_v[:, :, bass.ds(g * D, D)]).then_inc(wk_in, 16)
                sp.wait_ge(wv_lo_d, g)
                sp.dma_start(wv_raw[:], wv_v[:, :, bass.ds(g * D, D)]).then_inc(wv_in, 16)
                sp.wait_ge(wq_lo_d, g * R)
                sp.dma_start(wq_raw[:], wq_v[:, :, bass.ds(g * (R * D), R * D)]).then_inc(wq_in, 16)
                sp.wait_ge(wo_lo_d, g * R)
                sp.dma_start(wo_raw[:], wo_v[:, bass.ds(g * R, R), :]).then_inc(wo_in, 16)
            sp.wait_ge(wq_lo_d, G * R)
            sp.dma_start(wb_raw[:], w_base.rearrange("(t p) h -> p t h", p=P)).then_inc(wb_in, 16)
            sp.wait_ge(wk_lo_d, G)
            sp.dma_start(la_raw[:].rearrange("p k d -> p (k d)"), lora_a.rearrange("e r h -> (e r) h")).then_inc(la_in, 16)
            sp.wait_ge(wv_lo_d, G)
            sp.dma_start(lb_raw[:].rearrange("p k d -> p (k d)").rearrange("p (e c) -> p e c", e=E),
                         lora_b.rearrange("e (p j) r -> p e (j r)", j=4)).then_inc(lb_in, 16)
            sp.wait_ge(acc_init, 1)
            sp.dma_start(row_bias[:], b_base.partition_broadcast(P)).then_inc(bb_in, 16)
            for i in range(NT):
                sp.wait_ge(h2_done, i + 1)
                sp.dma_start(out_v[:, i, :], acc[:, i, :]).then_inc(out_done, 16)
            sp.wait_ge(out_done, 16 * NT)

        @block.scalar
        def _(act):
            act.dma_start(ident[:], ident_t).then_inc(ident_in, 16)
            act.dma_start(bias_rows[0:H, :], bq.rearrange("(h d) -> h d", d=D)).then_inc(bias_in, 16)
            act.dma_start(bias_rows[H:H + G, :], bk.rearrange("(h d) -> h d", d=D)).then_inc(bias_in, 16)
            act.dma_start(bias_rows[H + G:H + 2 * G, :], bv.rearrange("(h d) -> h d", d=D)).then_inc(bias_in, 16)
            act.dma_start(cos_sb[:], cos_t).then_inc(rope_in, 16)
            act.dma_start(sin_sb[:], sin_t).then_inc(rope_in, 16)
            act.dma_start(prior_sb[:], prior.partition_broadcast(P)).then_inc(small_in, 16)
            act.dma_start(rb_sb[:], router_b.partition_broadcast(P)).then_inc(small_in, 16)
            act.dma_start(act_i[:], active.partition_broadcast(P)).then_inc(small_in, 16)
            act.dma_start(ids_sb[:], ids_t).then_inc(small_in, 16)
            act.dma_start(row_bias[:], bo.partition_broadcast(P)).then_inc(bo_in, 16)
            act.dma_start(rt_raw[:], router_w).then_inc(rt_in, 16)
            act.wait_ge(prior_eps, 1)
            act.activation(logit_c[:, 1, :], logit_c[:, 0, :], ACT.Ln).then_inc(ln_prior, 1)
            act.wait_ge(bias_tr, 1)
            act.activation(bias_cols[:], ps_out[:, 0:H + 2 * G], ACT.Copy).then_inc(bias_done, 1)
            for i in range(NT):
                act.wait_ge(tr_done, i + 1)
                act.activation(xT_hi[:, :, i * P:(i + 1) * P], ps_tr[i % 2][:].rearrange("p (k t) -> p k t", k=KT),
                               ACT.Copy).then_inc(tr_hi_d, 1)
            act.wait_ge(bias_done, 1)

            projs_due = act.alloc_register("projs_due")

            def projected(proj):
                if isinstance(proj, int):
                    wait(act, proj_done, proj + 1)
                else:
                    act.wait_ge(proj_done, projs_due)
                    act.reg_add(projs_due, projs_due, 1)

            def rotate(proj, rope, bank, slot, col):
                wait(act, rope_done, rope - 1)
                projected(proj)
                h = D // 2
                act.activation(rope_rot[0:h, slot, :], ps_proj[bank][h:D, :], ACT.Identity,
                               bias=bias_cols[h:D, bass.ds(col, 1)])
                act.activation(rope_rot[h:D, slot, :], ps_proj[bank][0:h, :], ACT.Identity,
                               bias=bias_cols[0:h, bass.ds(col, 1)]).then_inc(evac_done, 1)

            def step(g, n):
                prev, cur, nxt = has(g)
                if (cur if n else prev):
                    N, m = g * STEPS + (n - 1), (n - 1) % STEPS
                    b, h = m // R, m % R
                    wait(act, pv_done, N + 1)
                    if h == 0:
                        wait(act, wo_done, g * STEPS - (STEPS - TT) if b == 0 else g * STEPS)
                    act.activation(ctx_hi[:, b, h, :], ps_ctx[:], ACT.Copy).then_inc(ctx_hi_d, 1)
                if cur:
                    N, t = g * STEPS + n, tr_no(g, TR_P[n])
                    wait(act, pv_done, N)
                    wait(act, tr_done, t + 1)
                    act.activation(pT_hi[:, PT_T3:PT_T0], ps_tr[(1 + TR_P[n]) % 2][:], ACT.Copy).then_inc(tr_hi_d, 1)
                    wait(act, tr_done, t + 2)
                    act.activation(pT_hi[:, PT_T0:PT_T2], ps_tr[TR_P[n] % 2][:], ACT.Copy).then_inc(tr_hi_d, 1)
                has_q = cur if n < 6 else nxt
                if has_q:
                    m = (n + 2) % STEPS
                    col = g * R + m % R if n < 6 else g * R + (R + m % R)
                    rotate(proj_q(g, n), rope_q(g, n), bank_q(g, n), rope_slot(ROPE_Q[n] + q_shift(g, n)), col)
                if cur:
                    wait(act, tr_done, t + 3)
                    act.activation(pT_hi[:, PT_T2:PT_END], ps_tr[(1 + TR_P[n]) % 2][:, 0:256], ACT.Copy).then_inc(tr_hi_d, 1)
                has_s = cur if n < 7 else nxt
                slot = (n + 1) % 2

                def exps(i):
                    return act.activation(prob[:, slot, SCOL[i]:SCOL[i + 1]], prob[:, slot, SCOL[i]:SCOL[i + 1]],
                                          ACT.Exp, bias=negmax[:, slot, i:i + 1], scale=-1.0,
                                          accum_out=rowsum[:, slot, i:i + 1])
                V0 = (g * STEPS + n + 1) * SC_PER
                if has_s:
                    wait(act, max_done, V0 + 1)
                    exps(1)
                    exps(0)
                    wait(act, max_done, V0 + 2)
                    exps(2).then_inc(exp_done, 1)
                    wait(act, max_done, V0 + 3)
                    exps(3).then_inc(exp_done, 1)
                if n in (0, 4) and (cur if n == 0 else nxt):
                    col = g + H if n == 0 else g + (H + 1)
                    rotate(proj_kv(g, n), rope_k(g, n), bank_kv(g, n), rope_slot(ROPE_K[n] + kv_shift(g, n)), col)
                if n in (2, 6) and (cur if n == 2 else nxt):
                    wait(act, tr_done, (tr_no(g, TR_V[3]) if n == 6 else tr_no(g - 1, TR_V[7])) + 1)
                    projected(proj_kv(g, n))
                    col = g + (H + G) if n == 2 else g + (H + G + 1)
                    act.activation(vT[:], ps_proj[bank_kv(g, n)][:], ACT.Identity,
                                   bias=bias_cols[:, bass.ds(col, 1)]).then_inc(evac_done, 1)
                if (n == 1 and cur) or (n == 5 and nxt):
                    b, r = (1, rope_k(g, 0)) if n == 1 else (0, rope_k(g, 4))
                    sl = rope_slot(ROPE_K[n - 1] + kv_shift(g, n - 1))
                    wait(act, rope_done, r + 1)
                    wait(act, sc_done, g * (STEPS * SC_PER) + (0 if n == 1 else R * SC_PER))
                    act.activation(k_hi[:, b, :], rope_cos[:, sl, :], ACT.Copy).then_inc(qk_hi_d, 1)
                if has_q:
                    wait(act, rope_done, rope_q(g, n) + 1)
                    wait(act, sc_done, (g * STEPS + n + 1) * SC_PER)
                    act.activation(q_hi[:, n % 2, :], rope_cos[:, rope_slot(ROPE_Q[n] + q_shift(g, n)), :], ACT.Copy).then_inc(qk_hi_d, 1)
                if n in TR_V and (cur if n == 3 else nxt):
                    b = 1 if n == 3 else 0
                    wait(act, tr_done, tr_no(g, TR_V[n]) + 1)
                    wait(act, pv_done, g * STEPS + (0 if n == 3 else R))
                    act.activation(v_hi[:, b, :, :], ps_tr[(1 + TR_V[n]) % 2][:].rearrange("p (t d) -> p t d", t=TT),
                                   ACT.Copy).then_inc(tr_hi_d, 1)
                if cur and n == 3:
                    wait(act, wo_in, 16 * g + 16)
                    wait(act, wo_done, STEPS * g)
                    for h in range(R):
                        act.activation(wo_hi[:, h, :], wo_raw[:, h, :], ACT.Copy).then_inc(wo_hi_d, 1)
                if nxt and n == 2:
                    wait(act, wk_in, 16 * g + 32)
                    wait(act, proj_done, proj_kv(g, 0) + 1)
                    act.activation(wkv_hi[:, 0, :, :], wk_raw[:], ACT.Copy).then_inc(wk_hi_d, 1)
                if nxt and 4 <= n <= 5:
                    wait(act, wq_in, 16 * g + 32)
                    for h in (2 * (n - 4), 2 * (n - 4) + 1):
                        wait(act, proj_done, proj_q(g, h + 2) + 1)
                        act.activation(wq_hi[:, h, :, :], wq_raw[:, :, h * D:(h + 1) * D], ACT.Copy).then_inc(wq_hi_d, 1)
                if nxt and n == 4:
                    wait(act, wv_in, 16 * g + 32)
                    wait(act, proj_done, proj_kv(g, 2) + 1)
                    act.activation(wkv_hi[:, 1, :, :], wv_raw[:], ACT.Copy).then_inc(wv_hi_d, 1)

            for g in (-1, 0):
                for n in range(STEPS):
                    step(g, n)
            act.reg_mov(projs_due, proj_q(1, 0) + 1)
            with act.Fori(1, G - 1) as g:
                for n in range(STEPS):
                    step(g, n)
            for n in range(STEPS):
                step(G - 1, n)
            step(G, 0)

            def tr_view(i, width=512):
                wait(act, tr_done, i + 1)
                return ps_tr[i % 2][:, 0:width]
            for k in range(KT):
                act.activation(wbT_hi[:, k, :], tr_view(TR_TAIL + k), ACT.Copy).then_inc(tr_hi_d, 1)
            act.activation(ar_hi[:, :, 0:ER], tr_view(TR_TAIL + 4).rearrange("p (k c) -> p k c", k=KT),
                           ACT.Copy).then_inc(tr_hi_d, 1)
            act.activation(ar_hi[:, :, ER:ER + E], tr_view(TR_TAIL + 5, KT * E).rearrange("p (k c) -> p k c", k=KT),
                           ACT.Copy).then_inc(tr_hi_d, 1)
            act.activation(lbT_hi.rearrange("p (q j) -> p j q", j=4),
                           tr_view(TR_TAIL + 6).rearrange("p (j q) -> p j q", j=4), ACT.Copy).then_inc(tr_hi_d, 1)

            def x1T_hi(i):
                no = TR_TAIL + N_PREP + (0 if i == 0 else 2 * i - 1)
                act.activation(xT_hi[:, :, i * P:(i + 1) * P], tr_view(no).rearrange("p (k t) -> p k t", k=KT),
                               ACT.Copy).then_inc(tr_hi_d, 1)
            x1T_hi(0)
            for i in range(NT):
                if i + 1 < NT:
                    x1T_hi(i + 1)
                act.wait_ge(nmx_done, i + 1)
                act.activation(sm[:, i % 2, 1, :], sm[:, i % 2, 0, :], ACT.Exp, bias=sms[:, i % 2, 0:1],
                               scale=-1.0).then_inc(e_done, 1)
                no = TR_TAIL + N_PREP + (2 * i + 2 if i + 1 < NT else 2 * i + 1)
                act.activation(zT_hi[:, i % 2, :], tr_view(no, P), ACT.Copy).then_inc(tr_hi_d, 1)

        @block.gpsimd
        def _(pool):
            pool.memset(pT_hi[:, PT_ZERO:PT_T3].bitcast(F32), 0.0)
            pool.memset(pT_lo[:, PT_ZERO:PT_T3].bitcast(F32), 0.0).then_inc(zero_done, 1)
            pool.memset(neg_half[:], -0.5).then_inc(const_done, 1)

            def low(dst, full, high):
                return pool.tensor_tensor(dst, full, high.bitcast(F32), ALU.subtract)

            def sine(proj, r, slot):
                wait(pool, evac_done, proj + 1)
                pool.tensor_tensor(rope_rot[:, slot, :], rope_rot[:, slot, :], sin_sb[:], ALU.mult).then_inc(sin_done, 1)

            def step(g, n):
                prev, cur, nxt = has(g)
                has_k = (n == 1 and cur) or (n == 5 and nxt)
                if has_k:
                    r = rope_k(g, n - 1)
                    sl = rope_slot(ROPE_K[n - 1] + kv_shift(g, n - 1))
                    sine(proj_kv(g, n - 1), r, sl)
                has_q = cur if n < 6 else nxt
                if has_q:
                    sine(proj_q(g, n), rope_q(g, n), rope_slot(ROPE_Q[n] + q_shift(g, n)))
                if has_k:
                    b = 1 if n == 1 else 0
                    wait(pool, qk_hi_d, r + 1)
                    low(k_lo[:, b, :], rope_cos[:, sl, :], k_hi[:, b, :]).then_inc(qk_lo_d, 1)
                if has_q:
                    wait(pool, qk_hi_d, rope_q(g, n) + 1)
                    low(q_lo[:, n % 2, :], rope_cos[:, rope_slot(ROPE_Q[n] + q_shift(g, n)), :],
                        q_hi[:, n % 2, :]).then_inc(qk_lo_d, 1)
                if cur and n == 3:
                    for h in range(R):
                        wait(pool, wo_hi_d, g * R + h + 1)
                        low(wo_lo[:, h, :], wo_raw[:, h, :], wo_hi[:, h, :]).then_inc(wo_lo_d, 1)
                if nxt and n == 2:
                    wait(pool, wk_hi_d, g + 2)
                    low(wkv_lo[:, 0, :, :], wk_raw[:], wkv_hi[:, 0, :, :]).then_inc(wk_lo_d, 1)
                if nxt and 4 <= n <= 5:
                    for h in (2 * (n - 4), 2 * (n - 4) + 1):
                        wait(pool, wq_hi_d, g * R + (R + h + 1))
                        low(wq_lo[:, h, :, :], wq_raw[:, :, h * D:(h + 1) * D], wq_hi[:, h, :, :]).then_inc(wq_lo_d, 1)
                if nxt and n == 4:
                    wait(pool, wv_hi_d, g + 2)
                    low(wkv_lo[:, 1, :, :], wv_raw[:], wkv_hi[:, 1, :, :]).then_inc(wv_lo_d, 1)

            pool.wait_ge(rope_in, 32)
            for n in range(STEPS):
                step(-1, n)
            pool.wait_ge(bo_in, 16)
            pool.wait_ge(tr_done, NT)
            for i in range(NT):
                last = pool.tensor_tensor(acc[:, i, :], acc[:, i, :], row_bias[:], ALU.add)
            last.then_inc(acc_init, 1)
            for n in range(STEPS):
                step(0, n)
            with pool.Fori(1, G - 1) as g:
                for n in range(STEPS):
                    step(g, n)
            for n in range(STEPS):
                step(G - 1, n)

            pool.wait_ge(proj_done, proj_kv(G - 1, 2) + 1)
            pool.memset(ar_hi[:, :, ER + E:ARW].bitcast(F32), 0.0)
            pool.memset(ar_lo[:, :, ER + E:ARW].bitcast(F32), 0.0).then_inc(pad_done, 1)
            pool.wait_ge(lb_in, 16)
            pool.wait_ge(tr_done, tr_no(G - 1, TR_V[3]) + 1)
            pool.tensor_copy(lb_jer[:].rearrange("p (j e r) -> p e j r", j=4, e=E),
                             lb_raw[:].rearrange("p k d -> p (k d)").rearrange("p (e j r) -> p e j r", e=E, j=4)
                             ).then_inc(lb_sorted, 1)
            pool.wait_ge(bb_in, 16)
            pool.wait_ge(const_done, 1)

            def rstd0(c):
                pool.wait_ge(ve_done, c + 1)
                pool.tensor_tensor(lnst[:, c % 2, 9:10], lnst[:, c % 2, 8:9], neg_half[:], ALU.pow).then_inc(rstd_done, 1)
            rstd0(0)
            c = 1
            for i in range(NT):
                if i + 1 < NT:
                    rstd0(c)
                    c += 1
                pool.wait_ge(tr_done, TR_TAIL + N_PREP + (0 if i == 0 else 2 * i - 1) + 1)
                pool.tensor_tensor(acc[:, i, :], acc[:, i, :], row_bias[:], ALU.add).then_inc(x1b_done, 1)
                if i > 0:
                    rstd0(c)
                    c += 1
            rstd0(c)

        @block.vector
        def _(dve):
            chain = [0]

            def link(ins):
                chain[0] += 1
                ins.then_inc(dve_chain, 1)
                dve.wait_ge(dve_chain, chain[0])

            dve.wait_ge(small_in, 64)
            nc.vector.tensor_scalar(logit_c[:, 0, :], prior_sb[:], PRIOR_EPS, None, ALU.add).then_inc(prior_eps, 1)
            link(nc.vector.tensor_copy(act_f[:], act_i[:]))
            link(nc.vector.tensor_scalar(cnt[:, 0, :], ids_sb[:], act_f[:, 0:1], None, ALU.is_equal))
            for a in range(1, 4):
                link(nc.vector.scalar_tensor_tensor(cnt[:, a, :], ids_sb[:], act_f[:, a:a + 1], cnt[:, a - 1, :],
                                                    ALU.is_equal, ALU.add))
            link(nc.vector.tensor_scalar(cnt[:, 4, :], cnt[:, 3, :], 0.0, OFF, ALU.is_equal, ALU.mult))
            dve.wait_ge(ln_prior, 1)
            link(nc.vector.tensor_tensor(logit_c[:, 2, :], logit_c[:, 1, :], rb_sb[:], ALU.add))
            link(nc.vector.tensor_tensor(logit_c[:, 3, :], logit_c[:, 2, :], cnt[:, 4, :], ALU.add))
            n_const = chain[0]

            def low(dst, full, high):
                return nc.vector.tensor_tensor(dst, full, high.bitcast(F32), ALU.subtract)

            for i in range(NT):
                dve.wait_ge(tr_hi_d, i + 1)
                cols = slice(i * P, (i + 1) * P)
                low(xT_lo[:, :, cols], ps_tr[i % 2][:].rearrange("p (k t) -> p k t", k=KT),
                    xT_hi[:, :, cols]).then_inc(tr_lo_d, 1)
            dve.wait_ge(bias_done, 1)
            dve.wait_ge(rope_in, 32)
            dve.wait_ge(mask_in, 16)

            tiles_seen = dve.alloc_register("score_tiles")

            def rope_part1(proj, r, bank, slot, col):
                wait(dve, qk_lo_d, r - 1)
                wait(dve, evac_done, proj + 1)
                nc.vector.scalar_tensor_tensor(rope_cos[:, slot, :], ps_proj[bank][:], bias_cols[:, bass.ds(col, 1)],
                                               cos_sb[:], ALU.add, ALU.mult).then_inc(cos_done, 1)

            def rope_part2(r, slot):
                wait(dve, cos_done, r + 1)
                wait(dve, sin_done, r + 1)
                nc.vector.tensor_tensor(rope_cos[:, slot, :], rope_cos[:, slot, :], rope_rot[:, slot, :],
                                        ALU.add).then_inc(rope_done, 1)

            def step(g, n):
                prev, cur, nxt = has(g)
                N = g * STEPS + n
                if (cur if n else prev):
                    m = (n - 1) % STEPS
                    wait(dve, ctx_hi_d, N)
                    low(ctx_lo[:, m // R, m % R, :], ps_ctx[:], ctx_hi[:, m // R, m % R, :]).then_inc(ctx_lo_d, 1)
                if cur:
                    t = tr_no(g, TR_P[n])
                    wait(dve, tr_hi_d, t + 1)
                    low(pT_lo[:, PT_T3:PT_T0], ps_tr[(1 + TR_P[n]) % 2][:], pT_hi[:, PT_T3:PT_T0]).then_inc(tr_lo_d, 1)
                    wait(dve, tr_hi_d, t + 2)
                    low(pT_lo[:, PT_T0:PT_T2], ps_tr[TR_P[n] % 2][:], pT_hi[:, PT_T0:PT_T2]).then_inc(tr_lo_d, 1)
                has_k = (n == 1 and cur) or (n == 5 and nxt)
                if has_k:
                    k_slot = rope_slot(ROPE_K[n - 1] + kv_shift(g, n - 1))
                    col = g + H if n == 1 else g + (H + 1)
                    rope_part1(proj_kv(g, n - 1), rope_k(g, n - 1), bank_kv(g, n - 1), k_slot, col)
                if (prev if n <= R else cur):
                    add_tile(g * STEPS + (n - R - 1), (n - R - 1) % STEPS)
                if has_k:
                    rope_part2(rope_k(g, n - 1), k_slot)
                slot = (n + 1) % 2
                has_s = cur if n < 7 else nxt

                def masked(i, bank, at):
                    w = (i + 1) * P
                    return nc.vector.tensor_tensor_reduce(
                        out=prob[:, slot, SCOL[i]:SCOL[i + 1]], in0=ps_sc[bank][:, at:at + w], in1=mask_sb[:, S - w:S],
                        scale=-SCALE, scalar=BIG, op0=ALU.add, op1=ALU.min, accum_out=negmax[:, slot, i:i + 1])

                def tile_ready(v):
                    if isinstance(g, int):
                        wait(dve, sc_done, (N + 1) * SC_PER + v + 1)
                    else:
                        dve.wait_ge(sc_done, tiles_seen)
                        dve.reg_add(tiles_seen, tiles_seen, 1)
                if has_s:
                    tile_ready(0)
                    masked(1, (n + 1) % 2, 0)
                    masked(0, (n + 1) % 2, 256).then_inc(max_done, 1)
                    tile_ready(1)
                    masked(2, n % 2, 0).then_inc(max_done, 1)
                has_q = cur if n < 6 else nxt
                if has_q:
                    m = (n + 2) % STEPS
                    col = g * R + m % R if n < 6 else g * R + (R + m % R)
                    q_slot = rope_slot(ROPE_Q[n] + q_shift(g, n))
                    rope_part1(proj_q(g, n), rope_q(g, n), bank_q(g, n), q_slot, col)
                if cur:
                    wait(dve, tr_hi_d, t + 3)
                    low(pT_lo[:, PT_T2:PT_END], ps_tr[(1 + TR_P[n]) % 2][:, 0:256], pT_hi[:, PT_T2:PT_END]).then_inc(tr_lo_d, 1)
                if has_s:
                    tile_ready(2)
                    masked(3, (n + 1) % 2, 0).then_inc(max_done, 1)
                if has_q:
                    rope_part2(rope_q(g, n), q_slot)
                if has_s:
                    for part, (i0, i1) in enumerate(((0, TT - 1), (TT - 1, TT))):
                        wait(dve, exp_done, 2 * N + 3 + part)
                        nc.vector.reciprocal(rinv[:, slot, i0:i1], rowsum[:, slot, i0:i1]).then_inc(rinv_done, 1)
                        wait(dve, rinv_done, 2 * N + 3 + part)
                        for i in range(i0, i1):
                            last = nc.vector.tensor_scalar(prob[:, slot, SCOL[i]:SCOL[i + 1]],
                                                           prob[:, slot, SCOL[i]:SCOL[i + 1]],
                                                           rinv[:, slot, i:i + 1], None, ALU.mult)
                    last.then_inc(p_ready, 1)
                if n in TR_V and (cur if n == 3 else nxt):
                    b = 1 if n == 3 else 0
                    wait(dve, tr_hi_d, tr_no(g, TR_V[n]) + 1)
                    low(v_lo[:, b, :, :], ps_tr[(1 + TR_V[n]) % 2][:].rearrange("p (t d) -> p t d", t=TT),
                        v_hi[:, b, :, :]).then_inc(tr_lo_d, 1)

            def add_tile(w, tile):
                if isinstance(w, int) and w < NT:
                    wait(dve, acc_init, 1)
                wait(dve, wo_done, w + 1)
                nc.vector.tensor_tensor(acc[:, tile, :], acc[:, tile, :], ps_out[:], ALU.add).then_inc(acc_done, 1)

            for g in (-1, 0):
                for n in range(STEPS):
                    step(g, n)
            dve.reg_mov(tiles_seen, (STEPS + 1) * SC_PER + 1)
            with dve.Fori(1, G - 1) as g:
                for n in range(STEPS):
                    step(g, n)
            for n in range(STEPS):
                step(G - 1, n)
            step(G, 0)
            add_tile(STEPS * G - R, TT)

            def tr_low(no, dst, hi_src, view):
                dve.wait_ge(tr_hi_d, no + 1)
                low(dst, view, hi_src).then_inc(tr_lo_d, 1)

            def bank(no, width=512):
                return ps_tr[no % 2][:, 0:width]
            for k in range(KT):
                tr_low(TR_TAIL + k, wbT_lo[:, k, :], wbT_hi[:, k, :], bank(TR_TAIL + k))
            a, rt, lb = TR_TAIL + 4, TR_TAIL + 5, TR_TAIL + 6
            tr_low(a, ar_lo[:, :, 0:ER], ar_hi[:, :, 0:ER], bank(a).rearrange("p (k c) -> p k c", k=KT))
            tr_low(rt, ar_lo[:, :, ER:ER + E], ar_hi[:, :, ER:ER + E], bank(rt, KT * E).rearrange("p (k c) -> p k c", k=KT))
            tr_low(lb, lbT_lo.rearrange("p (q j) -> p j q", j=4), lbT_hi.rearrange("p (q j) -> p j q", j=4),
                   bank(lb).rearrange("p (j q) -> p j q", j=4))

            norms = [0]

            def layer_norm(i):
                c = norms[0]
                norms[0] += 1
                st = lnst[:, c % 2, :]
                link(nc.vector.bn_stats(st[:, 0:6], acc[:, i, :]))
                link(nc.vector.bn_aggr(st[:, 6:8], st[:, 0:6]))
                nc.vector.tensor_scalar(st[:, 8:9], st[:, 7:8], LN_EPS, None, ALU.add).then_inc(ve_done, 1)
                dve.wait_ge(rstd_done, c + 1)
                dve.wait_ge(ve_done, c + 1)
                link(nc.vector.tensor_tensor(st[:, 10:11], st[:, 8:9], st[:, 9:10], ALU.mult))
                link(nc.vector.tensor_tensor(st[:, 11:12], st[:, 10:11], st[:, 9:10], ALU.mult))
                link(nc.vector.tensor_scalar(st[:, 12:13], st[:, 11:12], -0.5, 1.5, ALU.mult, ALU.add))
                link(nc.vector.tensor_tensor(st[:, 13:14], st[:, 12:13], st[:, 9:10], ALU.mult))
                return nc.vector.tensor_scalar(acc[:, i, :], acc[:, i, :], st[:, 6:7], st[:, 13:14],
                                               ALU.subtract, ALU.mult)

            def x1_tile(i):
                dve.wait_ge(acc_done, STEPS * (G - 1) + i + 1)
                layer_norm(i).then_inc(ln_done, 1)

            def x1T_low(i):
                no = TR_TAIL + N_PREP + (0 if i == 0 else 2 * i - 1)
                cols = slice(i * P, (i + 1) * P)
                tr_low(no, xT_lo[:, :, cols], xT_hi[:, :, cols], bank(no).rearrange("p (k t) -> p k t", k=KT))

            def router(i):
                s, z = i % 2, ps_proj[i % 2]
                dve.wait_ge(z_done, i + 1)
                nc.vector.tensor_tensor_reduce(out=sm[:, s, 0, :], in0=z[:, ER:ER + E], in1=logit_c[:, 3, :],
                                               scale=-1.0, scalar=BIG, op0=ALU.add, op1=ALU.min,
                                               accum_out=sms[:, s, 0:1]).then_inc(nmx_done, 1)
                dve.wait_ge(e_done, i + 1)
                link(nc.vector.tensor_tensor_reduce(out=sm[:, s, 2, :], in0=sm[:, s, 1, :], in1=cnt[:, 3, :],
                                                    scale=1.0, scalar=0.0, op0=ALU.mult, op1=ALU.add,
                                                    accum_out=sms[:, s, 1:2]))
                link(nc.vector.reciprocal(sms[:, s, 2:3], sms[:, s, 1:2]))
                link(nc.vector.tensor_scalar(sm[:, s, 3, :], sm[:, s, 2, :], sms[:, s, 2:3], LORA_SCALING, ALU.mult, ALU.mult))
                nc.vector.tensor_tensor(zz[:, s, :].rearrange("p (e r) -> p e r", r=RANK),
                                        z[:, 0:ER].rearrange("p (e r) -> p e r", r=RANK),
                                        sm[:, s, 3, :].unsqueeze(2).to_broadcast([P, E, RANK]), ALU.mult).then_inc(zz_done, 1)

            def finish(i):
                dve.wait_ge(y_done, i + 1)
                dve.wait_ge(x1b_done, i + 1)
                link(nc.vector.tensor_tensor(acc[:, i, :], acc[:, i, :], ps_sc[i % 2][:], ALU.add))
                layer_norm(i).then_inc(h2_done, 1)

            x1_tile(0)
            x1T_low(0)
            for i in range(NT):
                if i + 1 < TT:
                    add_tile(STEPS * G - R + 1 + i, TT + 1 + i)
                if i + 1 < NT:
                    x1_tile(i + 1)
                    x1T_low(i + 1)
                router(i)
                no = TR_TAIL + N_PREP + (2 * i + 2 if i + 1 < NT else 2 * i + 1)
                tr_low(no, zT_lo[:, i % 2, :], zT_hi[:, i % 2, :], bank(no, P))
                if i > 0:
                    finish(i - 1)
            finish(NT - 1)

        @block.tensor
        def _(pe):
            pe.wait_ge(ident_in, 16)
            pe.wait_ge(bias_in, 48)
            nc.tensor.transpose(ps_out[:, 0:H + 2 * G], bias_rows[:], ident[0:H + 2 * G, 0:H + 2 * G]).then_inc(bias_tr, 1)
            for i in range(NT):
                if i % TT == 0:
                    pe.wait_ge(x_in[i // TT], 16)
                wait(pe, tr_lo_d, i - 1)
                for k in range(KT):
                    last = nc.tensor.transpose(ps_tr[i % 2][:, k * P:(k + 1) * P], acc[:, i, k * P:(k + 1) * P], ident[:])
                last.then_inc(tr_done, 1)

            def project(w_hi, w_lo, b, bank):
                cols = slice(b * S, (b + 1) * S)
                for k in range(KT):
                    last = three(ps_proj[bank][:], w_hi[:, k, :], w_lo[:, k, :], xT_hi[:, k, cols], xT_lo[:, k, cols],
                                 k == 0, k == KT - 1)
                last.then_inc(proj_done, 1)

            def tr_free(g, j):
                wait(pe, tr_lo_d, tr_no(g, j) - 1)

            def proj_bank_free(g, j, number):
                wait(pe, evac_done, number - 1)
                wait(pe, cos_done, ropes_before(g, j))

            def step(g, n):
                prev, cur, nxt = has(g)
                slot = n % 2

                def p_tile(t, i, at, bank):
                    c = SCOL[i] + t * P
                    return nc.tensor.transpose(ps_tr[bank][:, at:at + P], prob[:, slot, c:c + P], ident[:])
                if cur:
                    j = TR_P[n]
                    tr_free(g, j)
                    wait(pe, p_ready, g * STEPS + (n + 1))
                    p_tile(3, 3, 0, (1 + j) % 2)
                    for i in range(1, TT):
                        last = p_tile(1, i, i * P, (1 + j) % 2)
                    last.then_inc(tr_done, 1)
                    tr_free(g, j + 1)
                    for i in range(TT):
                        last = p_tile(0, i, i * P, j % 2)
                    last.then_inc(tr_done, 1)
                if cur if n < 6 else nxt:
                    m = (n + 2) % STEPS
                    b, h = m // R, m % R
                    proj_bank_free(g, PROJ_Q[n] + q_shift(g, n), proj_q(g, n))
                    if b == 0:
                        wait(pe, wq_lo_d, g * R + (R + h + 1) if n >= 6 else g * R + (h + 1))
                    project(wq_hi[:, h, :, :], wq_lo[:, h, :, :], b, bank_q(g, n))
                if cur:
                    tr_free(g, j + 2)
                    for i in range(2, TT):
                        last = p_tile(2, i, (i - 2) * P, (1 + j) % 2)
                    last.then_inc(tr_done, 1)
                has_s = cur if n < 7 else nxt
                m = (n + 1) % STEPS
                V0 = (g * STEPS + (n + 1)) * SC_PER

                def scores(i, bank, at):
                    w = max(P * (i + 1), 256)
                    q = slice(i * P, (i + 1) * P)
                    return three(ps_sc[bank][:, at:at + w], q_hi[:, m % 2, q], q_lo[:, m % 2, q],
                                 k_hi[:, m // R, 0:w], k_lo[:, m // R, 0:w], True, True)
                if has_s:
                    wait(pe, qk_lo_d, (rope_q(g, n - 1) if n else rope_q(g - 1, 7)) + 1)
                    wait(pe, max_done, V0 - 1)
                    scores(1, m % 2, 0)
                    scores(0, m % 2, 256).then_inc(sc_done, 1)
                    wait(pe, max_done, V0)
                    scores(2, (m + 1) % 2, 0).then_inc(sc_done, 1)
                if n % 2 == 0 and (cur if n < 4 else nxt):
                    proj_bank_free(g, PROJ_KV[n] + kv_shift(g, n), proj_kv(g, n))
                    which = 0 if n in (0, 4) else 1
                    wait(pe, wk_lo_d if which == 0 else wv_lo_d, g + (1 if n < 4 else 2))
                    if isinstance(g, int) and g < 0 and n == 4:
                        wait(pe, tr_lo_d, TT)
                    project(wkv_hi[:, which, :, :], wkv_lo[:, which, :, :], 1 if n < 4 else 0, bank_kv(g, n))
                has_out = prev if n <= 3 else cur
                ahead = 1 if n % 2 else 0
                if has_out:
                    out_heads(g, n, 0, ahead)
                if has_s:
                    wait(pe, max_done, V0 + 1)
                    scores(3, m % 2, 0).then_inc(sc_done, 1)
                if has_out:
                    out_heads(g, n, ahead, R)
                if n in TR_V and (cur if n == 3 else nxt):
                    wait(pe, evac_done, proj_kv(g, n - 1) + 1)
                    tr_free(g, TR_V[n])
                    for t in range(TT):
                        last = nc.tensor.transpose(ps_tr[(1 + TR_V[n]) % 2][:, t * P:(t + 1) * P], vT[:, t * P:(t + 1) * P], ident[:])
                    last.then_inc(tr_done, 1)
                if cur:
                    N, b = g * STEPS + n, n // R
                    wait(pe, ctx_lo_d, N)
                    wait(pe, tr_lo_d, tr_no(g, TR_P[n]) + 3)
                    for t, s0, c in ((0, 0, PT_T0), (1, 128, PT_T1), (2, 256, PT_T2), (3, 256, PT_ZERO)):
                        w = S - s0
                        last = three(ps_ctx[:, s0:S], v_hi[:, b, t, :], v_lo[:, b, t, :], pT_hi[:, c:c + w], pT_lo[:, c:c + w],
                                     t == 0, t == TT - 1)
                    last.then_inc(pv_done, 1)

            def out_heads(g, n, h0, h1):
                w, m = g * STEPS + (n - R), (n - R) % STEPS
                b, t = m // TT, m % TT
                if h0 == 0 and h1 > 0:
                    wait(pe, acc_done, w)
                    if t == 0:
                        wait(pe, ctx_lo_d, g * STEPS + (R if b == 0 else 0))
                for h in range(h0, h1):
                    if m == 0:
                        wait(pe, wo_lo_d, g * R + (h + 1))
                    c = slice(t * P, (t + 1) * P)
                    last = three(ps_out[:], ctx_hi[:, b, h, c], ctx_lo[:, b, h, c], wo_hi[:, h, :], wo_lo[:, h, :],
                                 h == 0, h == R - 1)
                if h1 == R:
                    last.then_inc(wo_done, 1)

            for n in range(STEPS):
                step(-1, n)
            pe.wait_ge(bias_done, 1)
            pe.wait_ge(zero_done, 1)
            for n in range(STEPS):
                step(0, n)
            with pe.Fori(1, G - 1) as g:
                for n in range(STEPS):
                    step(g, n)
            for n in range(STEPS):
                step(G - 1, n)
            step(G, 0)

            pe.wait_ge(wb_in, 16)
            for k in range(KT):
                no = TR_TAIL + k
                wait(pe, tr_lo_d, no - 1)
                for t in range(HID // P):
                    last = nc.tensor.transpose(ps_tr[no % 2][:, t * P:(t + 1) * P], wb_raw[:, t, k * P:(k + 1) * P], ident[:])
                last.then_inc(tr_done, 1)
            no = TR_TAIL + 4
            pe.wait_ge(la_in, 16)
            wait(pe, tr_lo_d, no - 1)
            for k in range(KT):
                last = nc.tensor.transpose(ps_tr[no % 2][:, k * P:(k + 1) * P], la_raw[:, k, :], ident[:])
            last.then_inc(tr_done, 1)
            no = TR_TAIL + 5
            pe.wait_ge(rt_in, 16)
            wait(pe, tr_lo_d, no - 1)
            for k in range(KT):
                last = nc.tensor.transpose(ps_tr[no % 2][:, k * E:(k + 1) * E], rt_raw[:, k * P:(k + 1) * P], ident[0:E, 0:E])
            last.then_inc(tr_done, 1)
            no = TR_TAIL + 6
            pe.wait_ge(lb_sorted, 1)
            wait(pe, tr_lo_d, no - 1)
            for j in range(4):
                last = nc.tensor.transpose(ps_tr[no % 2][:, j * P:(j + 1) * P], lb_jer[:, j * ER:(j + 1) * ER], ident[:])
            last.then_inc(tr_done, 1)

            def x1_transpose(i):
                no = TR_TAIL + N_PREP + (0 if i == 0 else 2 * i - 1)
                pe.wait_ge(ln_done, i + 1)
                wait(pe, tr_lo_d, no - 1)
                for k in range(KT):
                    last = nc.tensor.transpose(ps_tr[no % 2][:, k * P:(k + 1) * P], acc[:, i, k * P:(k + 1) * P], ident[:])
                last.then_inc(tr_done, 1)

            def lora(i):
                no = TR_TAIL + N_PREP + (2 * i + 2 if i + 1 < NT else 2 * i + 1)
                wait(pe, tr_lo_d, no + 1)
                three(ps_sc[i % 2][:], zT_hi[:, i % 2, :], zT_lo[:, i % 2, :], lbT_hi, lbT_lo, False, True).then_inc(y_done, 1)

            x1_transpose(0)
            pe.wait_ge(pad_done, 1)
            for i in range(NT):
                if i + 1 < TT:
                    out_heads(G, 1 + i, 0, R)
                if i + 1 < NT:
                    x1_transpose(i + 1)
                no = TR_TAIL + N_PREP + (0 if i == 0 else 2 * i - 1)
                wait(pe, tr_lo_d, no + 1)
                wait(pe, zz_done, i - 1)
                c = slice(i * P, (i + 1) * P)
                for k in range(KT):
                    last = three(ps_proj[i % 2][:, 0:ARW], xT_hi[:, k, c], xT_lo[:, k, c], ar_hi[:, k, :], ar_lo[:, k, :],
                                 k == 0, k == KT - 1)
                last.then_inc(z_done, 1)
                if i > 0:
                    lora(i - 1)
                wait(pe, h2_done, i - 1)
                for k in range(KT):
                    three(ps_sc[i % 2][:], xT_hi[:, k, c], xT_lo[:, k, c], wbT_hi[:, k, :], wbT_lo[:, k, :], k == 0, False)
                no = TR_TAIL + N_PREP + (2 * i + 2 if i + 1 < NT else 2 * i + 1)
                pe.wait_ge(zz_done, i + 1)
                wait(pe, tr_lo_d, no - 1)
                nc.tensor.transpose(ps_tr[no % 2][:, 0:P], zz[:, i % 2, :], ident[:]).then_inc(tr_done, 1)
            lora(NT - 1)


_INS = ["attn_hidden_states", "attn_Wq", "attn_bq", "attn_Wk", "attn_bk", "attn_Wv", "attn_bv", "attn_Wo", "attn_bo",
        "ffn_W_base", "ffn_b_base", "ffn_lora_A", "ffn_lora_B", "ffn_router_W", "ffn_router_b", "ffn_domain_prior",
        "ffn_active"]


def _shape_constants():
    import numpy as np
    half = D // 2
    f = np.float32
    inv_freq = f(1.0) / np.power(f(10000.0), np.arange(half, dtype=f) / f(half))
    ang = np.arange(S, dtype=f)[None, :] * inv_freq[:, None].astype(f)
    cos, sin = np.cos(ang).astype(f), np.sin(ang).astype(f)
    mask = np.zeros((P, S), f)
    mask[:, S - P:] = np.where(np.arange(P)[None, :] > np.arange(P)[:, None], f(OFF), f(0))
    return {"cos": np.concatenate([cos, cos]), "sin": np.concatenate([-sin, sin]), "ident": np.eye(P, dtype=f),
            "mask": mask, "ids": np.tile(np.arange(E, dtype=f), (P, 1))}


def kernel(**inputs):
    import numpy as np
    import concourse.bacc as bacc
    from concourse.bass_utils import run_bass_kernel_spmd

    nc = bacc.Bacc("TRN2", target_bir_lowering=False, num_devices=1)
    arrays, args = {}, []
    data = [(n, np.ascontiguousarray(inputs["L0_" + n])) for n in _INS] + list(_shape_constants().items())
    for name, a in data:
        arrays[f"in_{name}"] = a
        args.append(nc.dram_tensor(f"in_{name}", a.shape, mybir.dt.from_np(a.dtype), kind="ExternalInput").ap())
    out = nc.dram_tensor("out_0", (B, S, HID), F32, kind="ExternalOutput").ap()
    layer_program(nc, *args, out)
    r = run_bass_kernel_spmd(nc, [arrays], core_ids=[0])
    return r.results[0]["out_0"]
```

```python
import concourse.bass as bass
from concourse import mybir
from contextlib import ExitStack

F32 = mybir.dt.float32
F32R = mybir.dt.float32r
I32 = mybir.dt.int32
ALU = mybir.AluOpType
ACT = mybir.ActivationFunctionType

P = 128
B, S, HID = 2, 512, 512
H, G, D = 32, 8, 128
R = H // G
KT = HID // P
TT = S // P
NT = B * TT
STEPS = B * R
E, RANK = 16, 8
ER = E * RANK
ARW = 256
SCALE = float(D) ** -0.5
LORA_SCALING = 16.0 / 8.0
LN_EPS = 1e-05
PRIOR_EPS = 1e-12
BIG = 3.0e38
OFF = -1.0e37

SCOL = [0, 128, 384, 768, 1280]
PT_ZERO, PT_T3, PT_T1, PT_T0, PT_T2, PT_END = 0, 128, 256, 640, 1152, 1408

PROJ_Q = [0, 2, 3, 5, 6, 8, 9, 11]
PROJ_KV = {0: 1, 2: 4, 4: 7, 6: 10}
PROJ_PER = 12
ROPES_UP_TO = [1, 2, 3, 4, 4, 5, 6, 7, 8, 9, 9, 10]
ROPE_Q = [0, 2, 3, 4, 5, 7, 8, 9]
ROPE_K = {0: 1, 4: 6}
ROPE_PER = 10
TR_P = [0, 3, 6, 9, 13, 16, 19, 22]
TR_V = {3: 12, 7: 25}
TR_PER = 26
TR_X = NT
SC_PER = 3
TR_ALL = TR_X + 1 + TR_PER * (G - 1) + 25
PREP_A, PREP_RT, PREP_LB, N_PREP = 4, 5, 6, 7
LATE_Z = NT


def kv_shift(g, n):
    return 1 if isinstance(g, int) and g < 0 and n == 4 else 0


def q_shift(g, n):
    return -1 if isinstance(g, int) and g == G - 1 and n == 5 else 0


def proj_q(g, n):
    return 4 + PROJ_PER * g + PROJ_Q[n] + q_shift(g, n)


def bank_q(g, n):
    return (PROJ_Q[n] + q_shift(g, n)) % 2


def bank_kv(g, n):
    return (PROJ_KV[n] + kv_shift(g, n)) % 2


def ropes_before(g, j):
    return 3 + ROPE_PER * g + (ROPES_UP_TO[j - 2] if j >= 2 else ROPES_UP_TO[j - 2] - ROPE_PER)


def proj_kv(g, n):
    return 4 + PROJ_PER * g + PROJ_KV[n] + kv_shift(g, n)


def rope_q(g, n):
    return 3 + ROPE_PER * g + ROPE_Q[n] + q_shift(g, n)


def rope_k(g, n):
    return 3 + ROPE_PER * g + ROPE_K[n] + kv_shift(g, n)


def rope_slot(j):
    return (3 + j) % 2


PROJ_ALL = proj_q(G - 1, 5) + 1
ROPE_ALL = rope_q(G - 1, 5) + 1


def tr_no(g, j):
    return TR_X + 1 + TR_PER * g + j


def layer_program(nc, x, wq, bq, wk, bk, wv, bv, wo, bo, w_base, b_base, lora_a, lora_b,
                  router_w, router_b, prior, active, cos_t, sin_t, ident_t, mask_t, ids_t, out):
    x_v = x.rearrange("b (t p) h -> p (b t) h", p=P)
    out_v = out.rearrange("b (t p) h -> p (b t) h", p=P)
    wq_v = wq.rearrange("(k p) n -> p k n", p=P)
    wk_v = wk.rearrange("(k p) n -> p k n", p=P)
    wv_v = wv.rearrange("(k p) n -> p k n", p=P)
    wo_v = wo.rearrange("(h d) n -> d h n", d=D)

    ctx = ExitStack()
    with ctx:
        def sb(name, shape, dt=F32):
            return ctx.enter_context(nc.sbuf_tensor(name, shape, dt))

        def ps(name):
            return ctx.enter_context(nc.psum_tensor(name, [P, 512], F32))

        def sem(name):
            return ctx.enter_context(nc.semaphore(name))

        xT_hi = sb("xT_hi", [P, KT, B * S], F32R)
        xT_lo = sb("xT_lo", [P, KT, B * S], F32R)
        acc = sb("acc", [P, NT, HID])
        wq_raw = sb("wq_raw", [P, KT, R * D])
        wk_raw = sb("wk_raw", [P, KT, D])
        wv_raw = sb("wv_raw", [P, KT, D])
        wo_raw = sb("wo_raw", [P, R, HID])
        wq_hi = sb("wq_hi", [P, R, KT, D], F32R)
        wq_lo = sb("wq_lo", [P, R, KT, D], F32R)
        wkv_hi = sb("wkv_hi", [P, 2, KT, D], F32R)
        wkv_lo = sb("wkv_lo", [P, 2, KT, D], F32R)
        wo_hi = sb("wo_hi", [P, R, HID], F32R)
        wo_lo = sb("wo_lo", [P, R, HID], F32R)
        k_hi = sb("k_hi", [P, B, S], F32R)
        k_lo = sb("k_lo", [P, B, S], F32R)
        v_hi = sb("v_hi", [P, B, TT, D], F32R)
        v_lo = sb("v_lo", [P, B, TT, D], F32R)
        q_hi = sb("q_hi", [P, 2, S], F32R)
        q_lo = sb("q_lo", [P, 2, S], F32R)
        rope_cos = sb("rope_cos", [P, 2, S])
        rope_rot = sb("rope_rot", [P, 2, S])
        vT = sb("vT", [P, S])
        prob = sb("prob", [P, 2, SCOL[4]])
        pT_hi = sb("pT_hi", [P, PT_END], F32R)
        pT_lo = sb("pT_lo", [P, PT_END], F32R)
        ctx_hi = sb("ctx_hi", [P, B, R, S], F32R)
        ctx_lo = sb("ctx_lo", [P, B, R, S], F32R)
        cos_sb = sb("cos_sb", [P, S])
        sin_sb = sb("sin_sb", [P, S])
        mask_sb = sb("mask_sb", [P, S])
        ident = sb("ident", [P, P])
        bias_rows = sb("bias_rows", [H + 2 * G, D])
        bias_cols = sb("bias_cols", [P, H + 2 * G])
        row_bias = sb("row_bias", [P, HID])
        negmax = sb("negmax", [P, 2, TT])
        rowsum = sb("rowsum", [P, 2, TT])
        rinv = sb("rinv", [P, 2, TT])
        rt_raw = sb("rt_raw", [E, HID])
        ids_sb = sb("ids_sb", [P, E])
        act_i = sb("act_i", [P, 4], I32)
        act_f = sb("act_f", [P, 4])
        cnt = sb("cnt", [P, 5, E])
        prior_sb = sb("prior_sb", [P, E])
        rb_sb = sb("rb_sb", [P, E])
        logit_c = sb("logit_c", [P, 4, E])
        neg_half = sb("neg_half", [P, TT])
        ln1_stats = sb("ln1_stats", [P, TT, 6])
        ln1_mv = sb("ln1_mv", [P, TT, 2])
        ln1_tmp = sb("ln1_tmp", [P, 6, TT])
        lnst = sb("lnst", [P, 2, 16])
        sms = sb("sms", [P, 3, TT])
        wb_raw, la_raw, lb_raw = wq_raw, wk_raw, wv_raw
        wbT_hi = wq_hi[:].rearrange("p r k d -> p r (k d)")
        wbT_lo = wq_lo[:].rearrange("p r k d -> p r (k d)")
        ar_hi = wkv_hi[:].rearrange("p a k d -> p (a k d)").rearrange("p (k c) -> p k c", c=ARW)
        ar_lo = wkv_lo[:].rearrange("p a k d -> p (a k d)").rearrange("p (k c) -> p k c", c=ARW)
        lbT_hi, lbT_lo = k_hi[:, 0, :], k_lo[:, 0, :]
        lb_jer = vT
        zz = rope_rot
        zT_hi, zT_lo = q_hi, q_lo
        sm = rope_cos[:, 0, 0:4 * TT * E].rearrange("p (s t e) -> p s t e", s=4, t=TT)

        ps_proj = [ps("ps_proj0"), ps("ps_proj1")]
        ps_sc = [ps("ps_sc0"), ps("ps_sc1")]
        ps_tr = [ps("ps_tr0"), ps("ps_tr1")]
        ps_ctx = ps("ps_ctx")
        ps_out = ps("ps_out")
        ps_y = [ps_sc[0], ps_sc[1], ps_out, ps_ctx]

        x_in = [sem("x_in0"), sem("x_in1")]
        ident_in, bias_in, rope_in, mask_in = sem("ident_in"), sem("bias_in"), sem("rope_in"), sem("mask_in")
        bo_in, small_in = sem("bo_in"), sem("small_in")
        wq_in, wk_in, wv_in, wo_in = sem("wq_in"), sem("wk_in"), sem("wv_in"), sem("wo_in")
        wb_in, la_in, lb_in, rt_in, bb_in = sem("wb_in"), sem("la_in"), sem("lb_in"), sem("rt_in"), sem("bb_in")
        out_done = sem("out_done")
        bias_tr, bias_done, acc_init = sem("bias_tr"), sem("bias_done"), sem("acc_init")
        zero_done, const_done = sem("zero_done"), sem("const_done")
        wq_hi_d, wq_lo_d = sem("wq_hi_d"), sem("wq_lo_d")
        wk_hi_d, wk_lo_d = sem("wk_hi_d"), sem("wk_lo_d")
        wv_hi_d, wv_lo_d = sem("wv_hi_d"), sem("wv_lo_d")
        wo_hi_d, wo_lo_d = sem("wo_hi_d"), sem("wo_lo_d")
        proj_done, evac_done = sem("proj_done"), sem("evac_done")
        cos_done, sin_done, rope_done = sem("cos_done"), sem("sin_done"), sem("rope_done")
        qk_hi_d, qk_lo_d = sem("qk_hi_d"), sem("qk_lo_d")
        sc_done, max_done, exp_done = sem("sc_done"), sem("max_done"), sem("exp_done")
        rinv_done, p_ready = sem("rinv_done"), sem("p_ready")
        tr_done, tr_hi_d, tr_lo_d = sem("tr_done"), sem("tr_hi_d"), sem("tr_lo_d")
        pv_done, ctx_hi_d, ctx_lo_d = sem("pv_done"), sem("ctx_hi_d"), sem("ctx_lo_d")
        wo_done, acc_done = sem("wo_done"), sem("acc_done")
        dve_chain, ln_done = sem("dve_chain"), sem("ln_done")
        stats_done, ve_done, rstd_done, x1b_done = sem("stats_done"), sem("ve_done"), sem("rstd_done"), sem("x1b_done")
        lb_sorted, pad_done, ln_prior, prior_eps = sem("lb_sorted"), sem("pad_done"), sem("ln_prior"), sem("prior_eps")
        z_done, nmx_done, e_done, zz_done = sem("z_done"), sem("nmx_done"), sem("e_done"), sem("zz_done")
        y_done, y_added, h2_done = sem("y_done"), sem("y_added"), sem("h2_done")
        prep_done, prep_hi_d, prep_lo_d = sem("prep_done"), sem("prep_hi_d"), sem("prep_lo_d")
        late_done, late_hi_d, late_lo_d = sem("late_done"), sem("late_hi_d"), sem("late_lo_d")

        def wait(eng, s, value):
            if isinstance(value, int) and value <= 0:
                return
            eng.wait_ge(s, value)

        def has(g):
            if not isinstance(g, int):
                return True, True, True
            return 1 <= g <= G, 0 <= g < G, g < G - 1

        def three(out_ap, w_hi, w_lo, m_hi, m_lo, first, last):
            nc.tensor.matmul(out_ap, w_hi, m_hi, start=first, stop=False)
            nc.tensor.matmul(out_ap, w_hi, m_lo, start=False, stop=False)
            return nc.tensor.matmul(out_ap, w_lo, m_hi, start=False, stop=last)

        def z_view(i):
            return ps_proj[(i % TT) // 2][:, (i % 2) * ARW:(i % 2 + 1) * ARW]

        def prep_view(k):
            full = ps_proj[k % 2][:]
            if k == PREP_RT:
                return full[:, 0:KT * E].rearrange("p (k c) -> p k c", k=KT)
            if k == PREP_A:
                return full.rearrange("p (k c) -> p k c", k=KT)
            return full.rearrange("p (j q) -> p j q", j=4) if k == PREP_LB else full

        def prep_dst(k, wbT, ar, lbT):
            if k == PREP_RT:
                return ar[:, :, ER:ER + E]
            if k == PREP_A:
                return ar[:, :, 0:ER]
            return lbT.rearrange("p (q j) -> p j q", j=4) if k == PREP_LB else wbT[:, k, :]

        def preps(g, n, place):
            return {(6, 0): (0, 1), (6, 1): (2,), (7, 0): (3, 4), (7, 1): (5, 6)}.get((n, place), ()) if (
                isinstance(g, int) and g == G - 1) else ()

        block = ctx.enter_context(nc.Block())

        @block.sync
        def _(sp):
            for b in range(B):
                sp.dma_start(acc[:, b * TT:(b + 1) * TT, :], x_v[:, b * TT:(b + 1) * TT, :]).then_inc(x_in[b], 16)
                if b == 0:
                    sp.dma_start(wk_raw[:], wk_v[:, :, 0:D]).then_inc(wk_in, 16)
                    sp.dma_start(wq_raw[:], wq_v[:, :, 0:R * D]).then_inc(wq_in, 16)
                    sp.dma_start(wv_raw[:], wv_v[:, :, 0:D]).then_inc(wv_in, 16)
            sp.dma_start(mask_sb[:], mask_t).then_inc(mask_in, 16)
            sp.dma_start(wo_raw[:], wo_v[:, 0:R, :]).then_inc(wo_in, 16)
            with sp.Fori(1, G) as g:
                sp.wait_ge(wk_lo_d, g)
                sp.dma_start(wk_raw[:], wk_v[:, :, bass.ds(g * D, D)]).then_inc(wk_in, 16)
                sp.wait_ge(wv_lo_d, g)
                sp.dma_start(wv_raw[:], wv_v[:, :, bass.ds(g * D, D)]).then_inc(wv_in, 16)
                sp.wait_ge(wq_lo_d, g * R)
                sp.dma_start(wq_raw[:], wq_v[:, :, bass.ds(g * (R * D), R * D)]).then_inc(wq_in, 16)
                sp.wait_ge(wo_lo_d, g * R)
                sp.dma_start(wo_raw[:], wo_v[:, bass.ds(g * R, R), :]).then_inc(wo_in, 16)
            sp.wait_ge(wq_lo_d, G * R)
            sp.dma_start(wb_raw[:], w_base.rearrange("(t p) h -> p t h", p=P)).then_inc(wb_in, 16)
            sp.wait_ge(wk_lo_d, G)
            sp.dma_start(la_raw[:].rearrange("p k d -> p (k d)"), lora_a.rearrange("e r h -> (e r) h")).then_inc(la_in, 16)
            sp.wait_ge(wv_lo_d, G)
            sp.dma_start(lb_raw[:].rearrange("p k d -> p (k d)").rearrange("p (e c) -> p e c", e=E),
                         lora_b.rearrange("e (p j) r -> p e (j r)", j=4)).then_inc(lb_in, 16)
            sp.wait_ge(acc_init, 1)
            sp.dma_start(row_bias[:], b_base.partition_broadcast(P)).then_inc(bb_in, 16)
            for i in range(NT):
                sp.wait_ge(h2_done, i + 1)
                sp.dma_start(out_v[:, i, :], acc[:, i, :]).then_inc(out_done, 16)
            sp.wait_ge(out_done, 16 * NT)

        @block.scalar
        def _(act):
            act.dma_start(ident[:], ident_t).then_inc(ident_in, 16)
            act.dma_start(bias_rows[0:H, :], bq.rearrange("(h d) -> h d", d=D)).then_inc(bias_in, 16)
            act.dma_start(bias_rows[H:H + G, :], bk.rearrange("(h d) -> h d", d=D)).then_inc(bias_in, 16)
            act.dma_start(bias_rows[H + G:H + 2 * G, :], bv.rearrange("(h d) -> h d", d=D)).then_inc(bias_in, 16)
            act.dma_start(cos_sb[:], cos_t).then_inc(rope_in, 16)
            act.dma_start(sin_sb[:], sin_t).then_inc(rope_in, 16)
            act.dma_start(prior_sb[:], prior.partition_broadcast(P)).then_inc(small_in, 16)
            act.dma_start(rb_sb[:], router_b.partition_broadcast(P)).then_inc(small_in, 16)
            act.dma_start(act_i[:], active.partition_broadcast(P)).then_inc(small_in, 16)
            act.dma_start(ids_sb[:], ids_t).then_inc(small_in, 16)
            act.dma_start(row_bias[:], bo.partition_broadcast(P)).then_inc(bo_in, 16)
            act.dma_start(rt_raw[:], router_w).then_inc(rt_in, 16)
            act.wait_ge(prior_eps, 1)
            act.activation(logit_c[:, 1, :], logit_c[:, 0, :], ACT.Ln).then_inc(ln_prior, 1)
            act.wait_ge(bias_tr, 1)
            act.activation(bias_cols[:], ps_out[:, 0:H + 2 * G], ACT.Copy).then_inc(bias_done, 1)
            for i in range(NT):
                act.wait_ge(tr_done, i + 1)
                act.activation(xT_hi[:, :, i * P:(i + 1) * P], ps_tr[i % 2][:].rearrange("p (k t) -> p k t", k=KT),
                               ACT.Copy).then_inc(tr_hi_d, 1)
            act.wait_ge(bias_done, 1)

            projs_due = act.alloc_register("projs_due")

            def projected(proj):
                if isinstance(proj, int):
                    wait(act, proj_done, proj + 1)
                else:
                    act.wait_ge(proj_done, projs_due)
                    act.reg_add(projs_due, projs_due, 1)

            def rotate(proj, rope, bank, slot, col):
                wait(act, rope_done, rope - 1)
                projected(proj)
                h = D // 2
                act.activation(rope_rot[0:h, slot, :], ps_proj[bank][h:D, :], ACT.Identity,
                               bias=bias_cols[h:D, bass.ds(col, 1)])
                act.activation(rope_rot[h:D, slot, :], ps_proj[bank][0:h, :], ACT.Identity,
                               bias=bias_cols[0:h, bass.ds(col, 1)]).then_inc(evac_done, 1)

            def prep_hi(k):
                wait(act, prep_done, k + 1)
                act.activation(prep_dst(k, wbT_hi, ar_hi, lbT_hi), prep_view(k), ACT.Copy).then_inc(prep_hi_d, 1)

            def step(g, n):
                prev, cur, nxt = has(g)
                if (cur if n else prev):
                    N, m = g * STEPS + (n - 1), (n - 1) % STEPS
                    b, h = m // R, m % R
                    wait(act, pv_done, N + 1)
                    if h == 0:
                        wait(act, wo_done, g * STEPS - (STEPS - TT) if b == 0 else g * STEPS)
                    act.activation(ctx_hi[:, b, h, :], ps_ctx[:], ACT.Copy).then_inc(ctx_hi_d, 1)
                if cur:
                    N, t = g * STEPS + n, tr_no(g, TR_P[n])
                    wait(act, pv_done, N)
                    wait(act, tr_done, t + 1)
                    act.activation(pT_hi[:, PT_T3:PT_T0], ps_tr[(1 + TR_P[n]) % 2][:], ACT.Copy).then_inc(tr_hi_d, 1)
                    wait(act, tr_done, t + 2)
                    act.activation(pT_hi[:, PT_T0:PT_T2], ps_tr[TR_P[n] % 2][:], ACT.Copy).then_inc(tr_hi_d, 1)
                has_q = cur if n < 6 else nxt
                if has_q:
                    m = (n + 2) % STEPS
                    col = g * R + m % R if n < 6 else g * R + (R + m % R)
                    rotate(proj_q(g, n), rope_q(g, n), bank_q(g, n), rope_slot(ROPE_Q[n] + q_shift(g, n)), col)
                for k in preps(g, n, 0):
                    prep_hi(k)
                if cur:
                    wait(act, tr_done, t + 3)
                    act.activation(pT_hi[:, PT_T2:PT_END], ps_tr[(1 + TR_P[n]) % 2][:, 0:256], ACT.Copy).then_inc(tr_hi_d, 1)
                has_s = cur if n < 7 else nxt
                slot = (n + 1) % 2

                def exps(i):
                    return act.activation(prob[:, slot, SCOL[i]:SCOL[i + 1]], prob[:, slot, SCOL[i]:SCOL[i + 1]],
                                          ACT.Exp, bias=negmax[:, slot, i:i + 1], scale=-1.0,
                                          accum_out=rowsum[:, slot, i:i + 1])
                V0 = (g * STEPS + n + 1) * SC_PER
                if has_s:
                    wait(act, max_done, V0 + 1)
                    exps(1)
                    exps(0)
                    wait(act, max_done, V0 + 2)
                    exps(2).then_inc(exp_done, 1)
                    wait(act, max_done, V0 + 3)
                    exps(3).then_inc(exp_done, 1)
                for k in preps(g, n, 1):
                    prep_hi(k)
                if n in (0, 4) and (cur if n == 0 else nxt):
                    col = g + H if n == 0 else g + (H + 1)
                    rotate(proj_kv(g, n), rope_k(g, n), bank_kv(g, n), rope_slot(ROPE_K[n] + kv_shift(g, n)), col)
                if n in (2, 6) and (cur if n == 2 else nxt):
                    wait(act, tr_done, (tr_no(g, TR_V[3]) if n == 6 else tr_no(g - 1, TR_V[7])) + 1)
                    projected(proj_kv(g, n))
                    col = g + (H + G) if n == 2 else g + (H + G + 1)
                    act.activation(vT[:], ps_proj[bank_kv(g, n)][:], ACT.Identity,
                                   bias=bias_cols[:, bass.ds(col, 1)]).then_inc(evac_done, 1)
                if (n == 1 and cur) or (n == 5 and nxt):
                    b, r = (1, rope_k(g, 0)) if n == 1 else (0, rope_k(g, 4))
                    sl = rope_slot(ROPE_K[n - 1] + kv_shift(g, n - 1))
                    wait(act, rope_done, r + 1)
                    wait(act, sc_done, g * (STEPS * SC_PER) + (0 if n == 1 else R * SC_PER))
                    act.activation(k_hi[:, b, :], rope_cos[:, sl, :], ACT.Copy).then_inc(qk_hi_d, 1)
                if has_q:
                    wait(act, rope_done, rope_q(g, n) + 1)
                    wait(act, sc_done, (g * STEPS + n + 1) * SC_PER)
                    act.activation(q_hi[:, n % 2, :], rope_cos[:, rope_slot(ROPE_Q[n] + q_shift(g, n)), :], ACT.Copy).then_inc(qk_hi_d, 1)
                if n in TR_V and (cur if n == 3 else nxt):
                    b = 1 if n == 3 else 0
                    wait(act, tr_done, tr_no(g, TR_V[n]) + 1)
                    wait(act, pv_done, g * STEPS + (0 if n == 3 else R))
                    act.activation(v_hi[:, b, :, :], ps_tr[(1 + TR_V[n]) % 2][:].rearrange("p (t d) -> p t d", t=TT),
                                   ACT.Copy).then_inc(tr_hi_d, 1)
                if cur and n == 3:
                    wait(act, wo_in, 16 * g + 16)
                    wait(act, wo_done, STEPS * g)
                    for h in range(R):
                        act.activation(wo_hi[:, h, :], wo_raw[:, h, :], ACT.Copy).then_inc(wo_hi_d, 1)
                if nxt and n == 2:
                    wait(act, wk_in, 16 * g + 32)
                    wait(act, proj_done, proj_kv(g, 0) + 1)
                    act.activation(wkv_hi[:, 0, :, :], wk_raw[:], ACT.Copy).then_inc(wk_hi_d, 1)
                if nxt and 4 <= n <= 5:
                    wait(act, wq_in, 16 * g + 32)
                    for h in (2 * (n - 4), 2 * (n - 4) + 1):
                        wait(act, proj_done, proj_q(g, h + 2) + 1)
                        act.activation(wq_hi[:, h, :, :], wq_raw[:, :, h * D:(h + 1) * D], ACT.Copy).then_inc(wq_hi_d, 1)
                if nxt and n == 4:
                    wait(act, wv_in, 16 * g + 32)
                    wait(act, proj_done, proj_kv(g, 2) + 1)
                    act.activation(wkv_hi[:, 1, :, :], wv_raw[:], ACT.Copy).then_inc(wv_hi_d, 1)

            for g in (-1, 0):
                for n in range(STEPS):
                    step(g, n)
            act.reg_mov(projs_due, proj_q(1, 0) + 1)
            with act.Fori(1, G - 1) as g:
                for n in range(STEPS):
                    step(g, n)
            for n in range(STEPS):
                step(G - 1, n)
            step(G, 0)

            def x1T_hi(i):
                act.wait_ge(late_done, i + 1)
                act.activation(xT_hi[:, :, i * P:(i + 1) * P], ps_tr[i % 2][:].rearrange("p (k t) -> p k t", k=KT),
                               ACT.Copy).then_inc(late_hi_d, 1)

            def zT_high(b):
                act.wait_ge(late_done, LATE_Z + b + 1)
                act.activation(zT_hi[:, b, :], ps_tr[b][:], ACT.Copy).then_inc(late_hi_d, 1)

            def router_exps(b):
                act.wait_ge(nmx_done, b + 1)
                for t in range(TT):
                    last = act.activation(sm[:, 1, t, :], sm[:, 0, t, :], ACT.Exp, bias=sms[:, 0, t:t + 1], scale=-1.0)
                last.then_inc(e_done, 1)
            for i in range(TT):
                x1T_hi(i)
            router_exps(0)
            for i in range(TT, NT):
                x1T_hi(i)
            zT_high(0)
            router_exps(1)
            zT_high(1)

        @block.gpsimd
        def _(pool):
            pool.memset(pT_hi[:, PT_ZERO:PT_T3].bitcast(F32), 0.0)
            pool.memset(pT_lo[:, PT_ZERO:PT_T3].bitcast(F32), 0.0).then_inc(zero_done, 1)
            pool.memset(neg_half[:], -0.5).then_inc(const_done, 1)

            def low(dst, full, high):
                return pool.tensor_tensor(dst, full, high.bitcast(F32), ALU.subtract)

            def sine(proj, r, slot):
                wait(pool, evac_done, proj + 1)
                pool.tensor_tensor(rope_rot[:, slot, :], rope_rot[:, slot, :], sin_sb[:], ALU.mult).then_inc(sin_done, 1)

            def step(g, n):
                prev, cur, nxt = has(g)
                has_k = (n == 1 and cur) or (n == 5 and nxt)
                if has_k:
                    r = rope_k(g, n - 1)
                    sl = rope_slot(ROPE_K[n - 1] + kv_shift(g, n - 1))
                    sine(proj_kv(g, n - 1), r, sl)
                has_q = cur if n < 6 else nxt
                if has_q:
                    sine(proj_q(g, n), rope_q(g, n), rope_slot(ROPE_Q[n] + q_shift(g, n)))
                if has_k:
                    b = 1 if n == 1 else 0
                    wait(pool, qk_hi_d, r + 1)
                    low(k_lo[:, b, :], rope_cos[:, sl, :], k_hi[:, b, :]).then_inc(qk_lo_d, 1)
                if has_q:
                    wait(pool, qk_hi_d, rope_q(g, n) + 1)
                    low(q_lo[:, n % 2, :], rope_cos[:, rope_slot(ROPE_Q[n] + q_shift(g, n)), :],
                        q_hi[:, n % 2, :]).then_inc(qk_lo_d, 1)
                if cur and n == 3:
                    for h in range(R):
                        wait(pool, wo_hi_d, g * R + h + 1)
                        low(wo_lo[:, h, :], wo_raw[:, h, :], wo_hi[:, h, :]).then_inc(wo_lo_d, 1)
                if nxt and n == 2:
                    wait(pool, wk_hi_d, g + 2)
                    low(wkv_lo[:, 0, :, :], wk_raw[:], wkv_hi[:, 0, :, :]).then_inc(wk_lo_d, 1)
                if nxt and 4 <= n <= 5:
                    for h in (2 * (n - 4), 2 * (n - 4) + 1):
                        wait(pool, wq_hi_d, g * R + (R + h + 1))
                        low(wq_lo[:, h, :, :], wq_raw[:, :, h * D:(h + 1) * D], wq_hi[:, h, :, :]).then_inc(wq_lo_d, 1)
                if isinstance(g, int) and g == G - 1 and n == 5:
                    pool.wait_ge(proj_done, proj_kv(g, 2) + 1)
                    pool.memset(ar_hi[:, :, ER + E:ARW].bitcast(F32), 0.0)
                    pool.memset(ar_lo[:, :, ER + E:ARW].bitcast(F32), 0.0).then_inc(pad_done, 1)
                    pool.wait_ge(lb_in, 16)
                    pool.wait_ge(tr_done, tr_no(g, TR_V[3]) + 1)
                    pool.tensor_copy(lb_jer[:].rearrange("p (j e r) -> p e j r", j=4, e=E),
                                     lb_raw[:].rearrange("p k d -> p (k d)").rearrange("p (e j r) -> p e j r", e=E, j=4)
                                     ).then_inc(lb_sorted, 1)
                if nxt and n == 4:
                    wait(pool, wv_hi_d, g + 2)
                    low(wkv_lo[:, 1, :, :], wv_raw[:], wkv_hi[:, 1, :, :]).then_inc(wv_lo_d, 1)

            pool.wait_ge(rope_in, 32)
            for n in range(STEPS):
                step(-1, n)
            pool.wait_ge(bo_in, 16)
            pool.wait_ge(tr_done, NT)
            for i in range(NT):
                last = pool.tensor_tensor(acc[:, i, :], acc[:, i, :], row_bias[:], ALU.add)
            last.then_inc(acc_init, 1)
            for n in range(STEPS):
                step(0, n)
            with pool.Fori(1, G - 1) as g:
                for n in range(STEPS):
                    step(g, n)
            for n in range(STEPS):
                step(G - 1, n)

            pool.wait_ge(bb_in, 16)
            pool.wait_ge(const_done, 1)

            def rstd(c, dst, var):
                pool.wait_ge(ve_done, c + 1)
                pool.tensor_tensor(dst, var, neg_half[:, 0:var.shape[-1]], ALU.pow).then_inc(rstd_done, 1)
            for b in range(B):
                rstd(b, ln1_tmp[:, 1, :], ln1_tmp[:, 0, :])
                for i in range(b * TT, (b + 1) * TT):
                    pool.wait_ge(late_done, i + 1)
                    pool.tensor_tensor(acc[:, i, :], acc[:, i, :], row_bias[:], ALU.add).then_inc(x1b_done, 1)
            for i in range(NT):
                rstd(B + i, lnst[:, i % 2, 9:10], lnst[:, i % 2, 8:9])

        @block.vector
        def _(dve):
            chain = [0]

            def link(ins):
                chain[0] += 1
                ins.then_inc(dve_chain, 1)
                dve.wait_ge(dve_chain, chain[0])

            dve.wait_ge(small_in, 64)
            nc.vector.tensor_scalar(logit_c[:, 0, :], prior_sb[:], PRIOR_EPS, None, ALU.add).then_inc(prior_eps, 1)
            link(nc.vector.tensor_copy(act_f[:], act_i[:]))
            link(nc.vector.tensor_scalar(cnt[:, 0, :], ids_sb[:], act_f[:, 0:1], None, ALU.is_equal))
            for a in range(1, 4):
                link(nc.vector.scalar_tensor_tensor(cnt[:, a, :], ids_sb[:], act_f[:, a:a + 1], cnt[:, a - 1, :],
                                                    ALU.is_equal, ALU.add))
            link(nc.vector.tensor_scalar(cnt[:, 4, :], cnt[:, 3, :], 0.0, OFF, ALU.is_equal, ALU.mult))
            dve.wait_ge(ln_prior, 1)
            link(nc.vector.tensor_tensor(logit_c[:, 2, :], logit_c[:, 1, :], rb_sb[:], ALU.add))
            link(nc.vector.tensor_tensor(logit_c[:, 3, :], logit_c[:, 2, :], cnt[:, 4, :], ALU.add))
            n_const = chain[0]

            def low(dst, full, high):
                return nc.vector.tensor_tensor(dst, full, high.bitcast(F32), ALU.subtract)

            for i in range(NT):
                dve.wait_ge(tr_hi_d, i + 1)
                cols = slice(i * P, (i + 1) * P)
                low(xT_lo[:, :, cols], ps_tr[i % 2][:].rearrange("p (k t) -> p k t", k=KT),
                    xT_hi[:, :, cols]).then_inc(tr_lo_d, 1)
            dve.wait_ge(bias_done, 1)
            dve.wait_ge(rope_in, 32)
            dve.wait_ge(mask_in, 16)

            tiles_seen = dve.alloc_register("score_tiles")

            def rope_part1(proj, r, bank, slot, col):
                wait(dve, qk_lo_d, r - 1)
                wait(dve, evac_done, proj + 1)
                nc.vector.scalar_tensor_tensor(rope_cos[:, slot, :], ps_proj[bank][:], bias_cols[:, bass.ds(col, 1)],
                                               cos_sb[:], ALU.add, ALU.mult).then_inc(cos_done, 1)

            def rope_part2(r, slot):
                wait(dve, cos_done, r + 1)
                wait(dve, sin_done, r + 1)
                nc.vector.tensor_tensor(rope_cos[:, slot, :], rope_cos[:, slot, :], rope_rot[:, slot, :],
                                        ALU.add).then_inc(rope_done, 1)

            def step(g, n):
                prev, cur, nxt = has(g)
                N = g * STEPS + n
                if (cur if n else prev):
                    m = (n - 1) % STEPS
                    wait(dve, ctx_hi_d, N)
                    low(ctx_lo[:, m // R, m % R, :], ps_ctx[:], ctx_hi[:, m // R, m % R, :]).then_inc(ctx_lo_d, 1)
                if cur:
                    t = tr_no(g, TR_P[n])
                    wait(dve, tr_hi_d, t + 1)
                    low(pT_lo[:, PT_T3:PT_T0], ps_tr[(1 + TR_P[n]) % 2][:], pT_hi[:, PT_T3:PT_T0]).then_inc(tr_lo_d, 1)
                    wait(dve, tr_hi_d, t + 2)
                    low(pT_lo[:, PT_T0:PT_T2], ps_tr[TR_P[n] % 2][:], pT_hi[:, PT_T0:PT_T2]).then_inc(tr_lo_d, 1)
                has_k = (n == 1 and cur) or (n == 5 and nxt)
                if has_k:
                    k_slot = rope_slot(ROPE_K[n - 1] + kv_shift(g, n - 1))
                    col = g + H if n == 1 else g + (H + 1)
                    rope_part1(proj_kv(g, n - 1), rope_k(g, n - 1), bank_kv(g, n - 1), k_slot, col)
                if (prev if n <= R else cur):
                    add_tile(g * STEPS + (n - R - 1), (n - R - 1) % STEPS)
                    if isinstance(g, int) and g * STEPS + (n - R - 1) >= STEPS * (G - 1):
                        tile_stats((n - R - 1) % STEPS)
                if has_k:
                    rope_part2(rope_k(g, n - 1), k_slot)
                slot = (n + 1) % 2
                has_s = cur if n < 7 else nxt

                def masked(i, bank, at):
                    w = (i + 1) * P
                    return nc.vector.tensor_tensor_reduce(
                        out=prob[:, slot, SCOL[i]:SCOL[i + 1]], in0=ps_sc[bank][:, at:at + w], in1=mask_sb[:, S - w:S],
                        scale=-SCALE, scalar=BIG, op0=ALU.add, op1=ALU.min, accum_out=negmax[:, slot, i:i + 1])

                def tile_ready(v):
                    if isinstance(g, int):
                        wait(dve, sc_done, (N + 1) * SC_PER + v + 1)
                    else:
                        dve.wait_ge(sc_done, tiles_seen)
                        dve.reg_add(tiles_seen, tiles_seen, 1)
                if has_s:
                    tile_ready(0)
                    masked(1, (n + 1) % 2, 0)
                    masked(0, (n + 1) % 2, 256).then_inc(max_done, 1)
                    tile_ready(1)
                    masked(2, n % 2, 0).then_inc(max_done, 1)
                has_q = cur if n < 6 else nxt
                if has_q:
                    m = (n + 2) % STEPS
                    col = g * R + m % R if n < 6 else g * R + (R + m % R)
                    q_slot = rope_slot(ROPE_Q[n] + q_shift(g, n))
                    rope_part1(proj_q(g, n), rope_q(g, n), bank_q(g, n), q_slot, col)
                for k in preps(g, n, 0):
                    prep_lo(k)
                if cur:
                    wait(dve, tr_hi_d, t + 3)
                    low(pT_lo[:, PT_T2:PT_END], ps_tr[(1 + TR_P[n]) % 2][:, 0:256], pT_hi[:, PT_T2:PT_END]).then_inc(tr_lo_d, 1)
                if has_s:
                    tile_ready(2)
                    masked(3, (n + 1) % 2, 0).then_inc(max_done, 1)
                if has_q:
                    rope_part2(rope_q(g, n), q_slot)
                if has_s:
                    for part, (i0, i1) in enumerate(((0, TT - 1), (TT - 1, TT))):
                        wait(dve, exp_done, 2 * N + 3 + part)
                        nc.vector.reciprocal(rinv[:, slot, i0:i1], rowsum[:, slot, i0:i1]).then_inc(rinv_done, 1)
                        wait(dve, rinv_done, 2 * N + 3 + part)
                        for i in range(i0, i1):
                            last = nc.vector.tensor_scalar(prob[:, slot, SCOL[i]:SCOL[i + 1]],
                                                           prob[:, slot, SCOL[i]:SCOL[i + 1]],
                                                           rinv[:, slot, i:i + 1], None, ALU.mult)
                    last.then_inc(p_ready, 1)
                for k in preps(g, n, 1):
                    prep_lo(k)
                if n in TR_V and (cur if n == 3 else nxt):
                    b = 1 if n == 3 else 0
                    wait(dve, tr_hi_d, tr_no(g, TR_V[n]) + 1)
                    low(v_lo[:, b, :, :], ps_tr[(1 + TR_V[n]) % 2][:].rearrange("p (t d) -> p t d", t=TT),
                        v_hi[:, b, :, :]).then_inc(tr_lo_d, 1)

            def prep_lo(k):
                wait(dve, prep_hi_d, k + 1)
                low(prep_dst(k, wbT_lo, ar_lo, lbT_lo), prep_view(k), prep_dst(k, wbT_hi, ar_hi, lbT_hi)).then_inc(prep_lo_d, 1)

            def tile_stats(i):
                dve.wait_ge(acc_done, STEPS * (G - 1) + i + 1)
                nc.vector.bn_stats(ln1_stats[:, i % TT, :], acc[:, i, :]).then_inc(stats_done, 1)

            def add_tile(w, tile, bank=None):
                if isinstance(w, int) and w < NT:
                    wait(dve, acc_init, 1)
                wait(dve, wo_done, w + 1)
                nc.vector.tensor_tensor(acc[:, tile, :], acc[:, tile, :], (bank or ps_out)[:], ALU.add).then_inc(acc_done, 1)

            for g in (-1, 0):
                for n in range(STEPS):
                    step(g, n)
            dve.reg_mov(tiles_seen, (STEPS + 1) * SC_PER + 1)
            with dve.Fori(1, G - 1) as g:
                for n in range(STEPS):
                    step(g, n)
            for n in range(STEPS):
                step(G - 1, n)
            step(G, 0)

            def newton(v, y, tmp):
                link(nc.vector.tensor_tensor(tmp[0], v, y, ALU.mult))
                link(nc.vector.tensor_tensor(tmp[1], tmp[0], y, ALU.mult))
                link(nc.vector.tensor_scalar(tmp[2], tmp[1], -0.5, 1.5, ALU.mult, ALU.add))
                link(nc.vector.tensor_tensor(tmp[3], tmp[2], y, ALU.mult))
                return tmp[3]

            def first_norm(b):
                dve.wait_ge(stats_done, (b + 1) * TT)
                for t in range(TT):
                    last = nc.vector.bn_aggr(ln1_mv[:, t, :], ln1_stats[:, t, :])
                link(last)
                nc.vector.tensor_scalar(ln1_tmp[:, 0, :], ln1_mv[:, :, 1], LN_EPS, None, ALU.add).then_inc(ve_done, 1)
                dve.wait_ge(rstd_done, b + 1)
                dve.wait_ge(ve_done, b + 1)
                r = newton(ln1_tmp[:, 0, :], ln1_tmp[:, 1, :], [ln1_tmp[:, j, :] for j in range(2, 6)])
                for t in range(TT):
                    i = b * TT + t
                    nc.vector.tensor_scalar(acc[:, i, :], acc[:, i, :], ln1_mv[:, t, 0:1], r[:, t:t + 1],
                                            ALU.subtract, ALU.mult).then_inc(ln_done, 1)

            def x1T_low(i):
                cols = slice(i * P, (i + 1) * P)
                dve.wait_ge(late_hi_d, i + 1)
                low(xT_lo[:, :, cols], ps_tr[i % 2][:].rearrange("p (k t) -> p k t", k=KT), xT_hi[:, :, cols]).then_inc(late_lo_d, 1)

            def zT_low(b):
                dve.wait_ge(late_hi_d, LATE_Z + b + 1)
                low(zT_lo[:, b, :], ps_tr[b][:], zT_hi[:, b, :]).then_inc(late_lo_d, 1)

            def router(b):
                dve.wait_ge(z_done, (b + 1) * TT)
                for t in range(TT):
                    last = nc.vector.tensor_tensor_reduce(out=sm[:, 0, t, :], in0=z_view(t)[:, ER:ER + E], in1=logit_c[:, 3, :],
                                                          scale=-1.0, scalar=BIG, op0=ALU.add, op1=ALU.min,
                                                          accum_out=sms[:, 0, t:t + 1])
                last.then_inc(nmx_done, 1)
                dve.wait_ge(e_done, b + 1)
                for t in range(TT):
                    last = nc.vector.tensor_tensor_reduce(out=sm[:, 2, t, :], in0=sm[:, 1, t, :], in1=cnt[:, 3, :],
                                                          scale=1.0, scalar=0.0, op0=ALU.mult, op1=ALU.add,
                                                          accum_out=sms[:, 1, t:t + 1])
                link(last)
                link(nc.vector.reciprocal(sms[:, 2, :], sms[:, 1, :]))
                for t in range(TT):
                    last = nc.vector.tensor_scalar(sm[:, 3, t, :], sm[:, 2, t, :], sms[:, 2, t:t + 1], LORA_SCALING,
                                                   ALU.mult, ALU.mult)
                link(last)
                for t in range(TT):
                    last = nc.vector.tensor_tensor(zz[:, b, t * ER:(t + 1) * ER].rearrange("p (e r) -> p e r", r=RANK),
                                                   z_view(t)[:, 0:ER].rearrange("p (e r) -> p e r", r=RANK),
                                                   sm[:, 3, t, :].unsqueeze(2).to_broadcast([P, E, RANK]), ALU.mult)
                last.then_inc(zz_done, 1)

            def finish_sum(i):
                st = lnst[:, i % 2, :]
                dve.wait_ge(y_done, i + 1)
                dve.wait_ge(x1b_done, i + 1)
                nc.vector.tensor_tensor(acc[:, i, :], acc[:, i, :], ps_y[i % TT][:], ALU.add).then_inc(y_added, 1)
                dve.wait_ge(y_added, i + 1)
                link(nc.vector.bn_stats(st[:, 0:6], acc[:, i, :]))
                link(nc.vector.bn_aggr(st[:, 6:8], st[:, 0:6]))
                nc.vector.tensor_scalar(st[:, 8:9], st[:, 7:8], LN_EPS, None, ALU.add).then_inc(ve_done, 1)

            def finish_norm(i):
                st = lnst[:, i % 2, :]
                dve.wait_ge(rstd_done, B + i + 1)
                dve.wait_ge(ve_done, B + i + 1)
                r = newton(st[:, 8:9], st[:, 9:10], [st[:, j:j + 1] for j in range(10, 14)])
                nc.vector.tensor_scalar(acc[:, i, :], acc[:, i, :], st[:, 6:7], r, ALU.subtract, ALU.mult).then_inc(h2_done, 1)

            def add_late(t):
                add_tile(STEPS * G - R + t, TT + t, ps_y[t])
                tile_stats(TT + t)

            first_norm(0)
            add_late(0)
            add_late(1)
            x1T_low(0)
            x1T_low(1)
            add_late(2)
            x1T_low(2)
            x1T_low(3)
            add_late(3)
            first_norm(1)
            router(0)
            for i in range(TT, NT):
                x1T_low(i)
            zT_low(0)
            finish_sum(0)
            finish_sum(1)
            finish_norm(0)
            router(1)
            zT_low(1)
            for i in range(2, NT):
                finish_sum(i)
                finish_norm(i - 1)
            finish_norm(NT - 1)

        @block.tensor
        def _(pe):
            pe.wait_ge(ident_in, 16)
            pe.wait_ge(bias_in, 48)
            nc.tensor.transpose(ps_out[:, 0:H + 2 * G], bias_rows[:], ident[0:H + 2 * G, 0:H + 2 * G]).then_inc(bias_tr, 1)
            for i in range(NT):
                if i % TT == 0:
                    pe.wait_ge(x_in[i // TT], 16)
                wait(pe, tr_lo_d, i - 1)
                for k in range(KT):
                    last = nc.tensor.transpose(ps_tr[i % 2][:, k * P:(k + 1) * P], acc[:, i, k * P:(k + 1) * P], ident[:])
                last.then_inc(tr_done, 1)

            def project(w_hi, w_lo, b, bank):
                cols = slice(b * S, (b + 1) * S)
                for k in range(KT):
                    last = three(ps_proj[bank][:], w_hi[:, k, :], w_lo[:, k, :], xT_hi[:, k, cols], xT_lo[:, k, cols],
                                 k == 0, k == KT - 1)
                last.then_inc(proj_done, 1)

            def tr_free(g, j):
                wait(pe, tr_lo_d, tr_no(g, j) - 1)

            def proj_bank_free(g, j, number):
                wait(pe, evac_done, number - 1)
                wait(pe, cos_done, ropes_before(g, j))

            def step(g, n):
                prev, cur, nxt = has(g)
                slot = n % 2

                def p_tile(t, i, at, bank):
                    c = SCOL[i] + t * P
                    return nc.tensor.transpose(ps_tr[bank][:, at:at + P], prob[:, slot, c:c + P], ident[:])
                if cur:
                    j = TR_P[n]
                    tr_free(g, j)
                    wait(pe, p_ready, g * STEPS + (n + 1))
                    p_tile(3, 3, 0, (1 + j) % 2)
                    for i in range(1, TT):
                        last = p_tile(1, i, i * P, (1 + j) % 2)
                    last.then_inc(tr_done, 1)
                    tr_free(g, j + 1)
                    for i in range(TT):
                        last = p_tile(0, i, i * P, j % 2)
                    last.then_inc(tr_done, 1)
                if cur if n < 6 else nxt:
                    m = (n + 2) % STEPS
                    b, h = m // R, m % R
                    proj_bank_free(g, PROJ_Q[n] + q_shift(g, n), proj_q(g, n))
                    if b == 0:
                        wait(pe, wq_lo_d, g * R + (R + h + 1) if n >= 6 else g * R + (h + 1))
                    project(wq_hi[:, h, :, :], wq_lo[:, h, :, :], b, bank_q(g, n))
                for k in preps(g, n, 0):
                    prep(k)
                if cur:
                    tr_free(g, j + 2)
                    for i in range(2, TT):
                        last = p_tile(2, i, (i - 2) * P, (1 + j) % 2)
                    last.then_inc(tr_done, 1)
                has_s = cur if n < 7 else nxt
                m = (n + 1) % STEPS
                V0 = (g * STEPS + (n + 1)) * SC_PER

                def scores(i, bank, at):
                    w = max(P * (i + 1), 256)
                    q = slice(i * P, (i + 1) * P)
                    return three(ps_sc[bank][:, at:at + w], q_hi[:, m % 2, q], q_lo[:, m % 2, q],
                                 k_hi[:, m // R, 0:w], k_lo[:, m // R, 0:w], True, True)
                if has_s:
                    wait(pe, qk_lo_d, (rope_q(g, n - 1) if n else rope_q(g - 1, 7)) + 1)
                    wait(pe, max_done, V0 - 1)
                    scores(1, m % 2, 0)
                    scores(0, m % 2, 256).then_inc(sc_done, 1)
                    wait(pe, max_done, V0)
                    scores(2, (m + 1) % 2, 0).then_inc(sc_done, 1)
                for k in preps(g, n, 1):
                    prep(k)
                if n % 2 == 0 and (cur if n < 4 else nxt):
                    proj_bank_free(g, PROJ_KV[n] + kv_shift(g, n), proj_kv(g, n))
                    which = 0 if n in (0, 4) else 1
                    wait(pe, wk_lo_d if which == 0 else wv_lo_d, g + (1 if n < 4 else 2))
                    if isinstance(g, int) and g < 0 and n == 4:
                        wait(pe, tr_lo_d, TT)
                    project(wkv_hi[:, which, :, :], wkv_lo[:, which, :, :], 1 if n < 4 else 0, bank_kv(g, n))
                has_out = prev if n <= 3 else cur
                ahead = 1 if n % 2 else 0
                if has_out:
                    out_heads(g, n, 0, ahead)
                if has_s:
                    wait(pe, max_done, V0 + 1)
                    scores(3, m % 2, 0).then_inc(sc_done, 1)
                if has_out:
                    out_heads(g, n, ahead, R)
                if n in TR_V and (cur if n == 3 else nxt):
                    wait(pe, evac_done, proj_kv(g, n - 1) + 1)
                    tr_free(g, TR_V[n])
                    for t in range(TT):
                        last = nc.tensor.transpose(ps_tr[(1 + TR_V[n]) % 2][:, t * P:(t + 1) * P], vT[:, t * P:(t + 1) * P], ident[:])
                    last.then_inc(tr_done, 1)
                if cur:
                    N, b = g * STEPS + n, n // R
                    wait(pe, ctx_lo_d, N)
                    wait(pe, tr_lo_d, tr_no(g, TR_P[n]) + 3)
                    for t, s0, c in ((0, 0, PT_T0), (1, 128, PT_T1), (2, 256, PT_T2), (3, 256, PT_ZERO)):
                        w = S - s0
                        last = three(ps_ctx[:, s0:S], v_hi[:, b, t, :], v_lo[:, b, t, :], pT_hi[:, c:c + w], pT_lo[:, c:c + w],
                                     t == 0, t == TT - 1)
                    last.then_inc(pv_done, 1)

            def out_heads(g, n, h0, h1, bank=None):
                w, m = g * STEPS + (n - R), (n - R) % STEPS
                b, t = m // TT, m % TT
                if h0 == 0 and h1 > 0 and bank is None:
                    wait(pe, acc_done, w)
                for h in range(h0, h1):
                    if t == 0:
                        wait(pe, ctx_lo_d, g * STEPS + (h + 1 if b == 0 else h + 1 - R))
                    if m == 0:
                        wait(pe, wo_lo_d, g * R + (h + 1))
                    c = slice(t * P, (t + 1) * P)
                    last = three((bank or ps_out)[:], ctx_hi[:, b, h, c], ctx_lo[:, b, h, c], wo_hi[:, h, :], wo_lo[:, h, :],
                                 h == 0, h == R - 1)
                if h1 == R:
                    last.then_inc(wo_done, 1)

            def prep(k):
                if k < 2:
                    wait(pe, evac_done, PROJ_ALL)
                    wait(pe, cos_done, ROPE_ALL)
                wait(pe, prep_lo_d, k - 1)
                bank = ps_proj[k % 2]
                if k < KT:
                    wait(pe, wb_in, 16)
                    for t in range(HID // P):
                        last = nc.tensor.transpose(bank[:, t * P:(t + 1) * P], wb_raw[:, t, k * P:(k + 1) * P], ident[:])
                elif k == PREP_A:
                    wait(pe, la_in, 16)
                    for k2 in range(KT):
                        last = nc.tensor.transpose(bank[:, k2 * P:(k2 + 1) * P], la_raw[:, k2, :], ident[:])
                elif k == PREP_RT:
                    wait(pe, rt_in, 16)
                    for k2 in range(KT):
                        last = nc.tensor.transpose(bank[:, k2 * E:(k2 + 1) * E], rt_raw[:, k2 * P:(k2 + 1) * P], ident[0:E, 0:E])
                else:
                    wait(pe, lb_sorted, 1)
                    for j in range(4):
                        last = nc.tensor.transpose(bank[:, j * P:(j + 1) * P], lb_jer[:, j * ER:(j + 1) * ER], ident[:])
                last.then_inc(prep_done, 1)

            for n in range(STEPS):
                step(-1, n)
            pe.wait_ge(bias_done, 1)
            pe.wait_ge(zero_done, 1)
            for n in range(STEPS):
                step(0, n)
            with pe.Fori(1, G - 1) as g:
                for n in range(STEPS):
                    step(g, n)
            for n in range(STEPS):
                step(G - 1, n)

            def x1_transpose(i):
                wait(pe, ln_done, i + 1)
                if i < 2:
                    wait(pe, tr_lo_d, TR_ALL)
                wait(pe, late_lo_d, i - 1)
                for k in range(KT):
                    last = nc.tensor.transpose(ps_tr[i % 2][:, k * P:(k + 1) * P], acc[:, i, k * P:(k + 1) * P], ident[:])
                last.then_inc(late_done, 1)

            def out_late(t):
                if t == 0:
                    wait(pe, max_done, STEPS * G * SC_PER)
                if t == 2:
                    wait(pe, acc_done, STEPS * G - R)
                if t == 3:
                    wait(pe, ctx_lo_d, STEPS * G)
                out_heads(G, t, 0, R, ps_y[t])

            def z_and_logits(i):
                if i == 0:
                    wait(pe, pad_done, 1)
                    wait(pe, prep_lo_d, N_PREP)
                if i == TT:
                    wait(pe, zz_done, 1)
                wait(pe, late_lo_d, i + 1)
                c = slice(i * P, (i + 1) * P)
                for k in range(KT):
                    last = three(z_view(i), xT_hi[:, k, c], xT_lo[:, k, c], ar_hi[:, k, :], ar_lo[:, k, :], k == 0, k == KT - 1)
                last.then_inc(z_done, 1)

            def dense(i):
                if i < TT:
                    wait(pe, acc_done, STEPS * G - R + i + 1)
                else:
                    wait(pe, y_added, i - TT + 1)
                c = slice(i * P, (i + 1) * P)
                for k in range(KT):
                    three(ps_y[i % TT][:], xT_hi[:, k, c], xT_lo[:, k, c], wbT_hi[:, k, :], wbT_lo[:, k, :], k == 0, False)

            def z_transpose(b):
                wait(pe, zz_done, b + 1)
                wait(pe, late_lo_d, LATE_Z + b - 1)
                for t in range(TT):
                    last = nc.tensor.transpose(ps_tr[b][:, t * P:(t + 1) * P], zz[:, b, t * ER:(t + 1) * ER], ident[:])
                last.then_inc(late_done, 1)

            def lora(i):
                b, c = i // TT, slice(i % TT * P, (i % TT + 1) * P)
                wait(pe, late_lo_d, LATE_Z + b + 1)
                three(ps_y[i % TT][:], zT_hi[:, b, c], zT_lo[:, b, c], lbT_hi, lbT_lo, False, True).then_inc(y_done, 1)

            for t in range(TT - 1):
                out_late(t)
            x1_transpose(0)
            x1_transpose(1)
            out_late(TT - 1)
            for i in range(2, TT):
                x1_transpose(i)
            for i in range(TT):
                z_and_logits(i)
            dense(0)
            x1_transpose(TT)
            x1_transpose(TT + 1)
            dense(1)
            x1_transpose(TT + 2)
            x1_transpose(TT + 3)
            z_transpose(0)
            for i in range(TT, NT):
                z_and_logits(i)
            lora(0)
            lora(1)
            dense(2)
            lora(2)
            dense(3)
            lora(3)
            z_transpose(1)
            for i in range(TT, NT):
                dense(i)
                lora(i)


_INS = ["attn_hidden_states", "attn_Wq", "attn_bq", "attn_Wk", "attn_bk", "attn_Wv", "attn_bv", "attn_Wo", "attn_bo",
        "ffn_W_base", "ffn_b_base", "ffn_lora_A", "ffn_lora_B", "ffn_router_W", "ffn_router_b", "ffn_domain_prior",
        "ffn_active"]


def _shape_constants():
    import numpy as np
    half = D // 2
    f = np.float32
    inv_freq = f(1.0) / np.power(f(10000.0), np.arange(half, dtype=f) / f(half))
    ang = np.arange(S, dtype=f)[None, :] * inv_freq[:, None].astype(f)
    cos, sin = np.cos(ang).astype(f), np.sin(ang).astype(f)
    mask = np.zeros((P, S), f)
    mask[:, S - P:] = np.where(np.arange(P)[None, :] > np.arange(P)[:, None], f(OFF), f(0))
    return {"cos": np.concatenate([cos, cos]), "sin": np.concatenate([-sin, sin]), "ident": np.eye(P, dtype=f),
            "mask": mask, "ids": np.tile(np.arange(E, dtype=f), (P, 1))}


def kernel(**inputs):
    import numpy as np
    import concourse.bacc as bacc
    from concourse.bass_utils import run_bass_kernel_spmd

    nc = bacc.Bacc("TRN2", target_bir_lowering=False, num_devices=1)
    arrays, args = {}, []
    data = [(n, np.ascontiguousarray(inputs["L0_" + n])) for n in _INS] + list(_shape_constants().items())
    for name, a in data:
        arrays[f"in_{name}"] = a
        args.append(nc.dram_tensor(f"in_{name}", a.shape, mybir.dt.from_np(a.dtype), kind="ExternalInput").ap())
    out = nc.dram_tensor("out_0", (B, S, HID), F32, kind="ExternalOutput").ap()
    layer_program(nc, *args, out)
    r = run_bass_kernel_spmd(nc, [arrays], core_ids=[0])
    return r.results[0]["out_0"]
```

```python
import concourse.bass as bass
from concourse import mybir
from contextlib import ExitStack

F32 = mybir.dt.float32
F32R = mybir.dt.float32r
I32 = mybir.dt.int32
ALU = mybir.AluOpType
ACT = mybir.ActivationFunctionType

P = 128
B, S, HID = 2, 512, 512
H, G, D = 32, 8, 128
R = H // G
KT = HID // P
TT = S // P
NT = B * TT
STEPS = B * R
E, RANK = 16, 8
N_ACTIVE = 4
ER = E * RANK
ARW = 256
SCALE = float(D) ** -0.5
LORA_SCALING = 16.0 / 8.0
LN_EPS = 1e-05
PRIOR_EPS = 1e-12
BIG = 3.0e38
OFF = -1.0e37

SCOL = [0, 128, 384, 768, 1280]
PT_T1, PT_T0, PT_T2, PT_END = 0, 384, 896, 1152

PROJ_Q = [0, 2, 3, 5, 6, 8, 9, 11]
PROJ_KV = {0: 1, 2: 4, 4: 7, 6: 10}
PROJ_PER = 12
ROPES_UP_TO = [1, 2, 3, 4, 4, 5, 6, 7, 8, 9, 9, 10]
ROPE_Q = [0, 2, 3, 4, 5, 7, 8, 9]
ROPE_K = {0: 1, 4: 6}
ROPE_PER = 10
TR_P = [0, 3, 6, 9, 13, 16, 19, 22]
TR_V = {3: 12, 7: 25}
TR_PER = 26
SC_PER = 3
TR_ALL = 1 + TR_PER * (G - 1) + 25
PREP_A, PREP_RT, PREP_LB, N_PREP = 4, 5, 6, 7
LATE_Z = NT


def kv_shift(g, n):
    return 1 if isinstance(g, int) and g < 0 and n == 4 else 0


def q_shift(g, n):
    return -1 if isinstance(g, int) and g == G - 1 and n == 5 else 0


def proj_q(g, n):
    return 4 + PROJ_PER * g + PROJ_Q[n] + q_shift(g, n)


def bank_q(g, n):
    return (PROJ_Q[n] + q_shift(g, n)) % 2


def bank_kv(g, n):
    return (PROJ_KV[n] + kv_shift(g, n)) % 2


def ropes_before(g, j):
    return 3 + ROPE_PER * g + (ROPES_UP_TO[j - 2] if j >= 2 else ROPES_UP_TO[j - 2] - ROPE_PER)


def proj_kv(g, n):
    return 4 + PROJ_PER * g + PROJ_KV[n] + kv_shift(g, n)


def rope_q(g, n):
    return 3 + ROPE_PER * g + ROPE_Q[n] + q_shift(g, n)


def rope_k(g, n):
    return 3 + ROPE_PER * g + ROPE_K[n] + kv_shift(g, n)


N_FIRST = 3


def rope_slot(j):
    return (3 + j) % 2


PROJ_ALL = proj_q(G - 1, 5) + 1
ROPE_ALL = rope_q(G - 1, 5) + 1


def tr_no(g, j):
    return 1 + TR_PER * g + j


def layer_program(nc, x, wq, bq, wk, bk, wv, bv, wo, bo, w_base, b_base, lora_a, lora_b,
                  router_w, router_b, prior, active, cos_t, sin_t, ident_t, mask_t, ids_t, out):
    x_v = x.rearrange("b (t p) h -> p (b t) h", p=P)
    out_v = out.rearrange("b (t p) h -> p (b t) h", p=P)
    wq_v = wq.rearrange("(k p) n -> p k n", p=P)
    wk_v = wk.rearrange("(k p) n -> p k n", p=P)
    wv_v = wv.rearrange("(k p) n -> p k n", p=P)
    wo_v = wo.rearrange("(h d) n -> d h n", d=D)

    ctx = ExitStack()
    with ctx:
        def sb(name, shape, dt=F32):
            return ctx.enter_context(nc.sbuf_tensor(name, shape, dt))

        def ps(name):
            return ctx.enter_context(nc.psum_tensor(name, [P, 512], F32))

        def sem(name):
            return ctx.enter_context(nc.semaphore(name))

        xT_hi = sb("xT_hi", [P, KT, B * S], F32R)
        xT_lo = sb("xT_lo", [P, KT, B * S], F32R)
        acc = sb("acc", [P, NT, HID])
        wq_raw = sb("wq_raw", [P, KT, R * D])
        wk_raw = sb("wk_raw", [P, KT, D])
        wv_raw = sb("wv_raw", [P, KT, D])
        wo_raw = sb("wo_raw", [P, R, HID])
        wq_hi = sb("wq_hi", [P, R, KT, D], F32R)
        wq_lo = sb("wq_lo", [P, R, KT, D], F32R)
        wkv_hi = sb("wkv_hi", [P, 2, KT, D], F32R)
        wkv_lo = sb("wkv_lo", [P, 2, KT, D], F32R)
        wo_hi = sb("wo_hi", [P, R, HID], F32R)
        wo_lo = sb("wo_lo", [P, R, HID], F32R)
        k_hi = sb("k_hi", [P, B, S], F32R)
        k_lo = sb("k_lo", [P, B, S], F32R)
        v_hi = sb("v_hi", [P, B, TT, D], F32R)
        v_lo = sb("v_lo", [P, B, TT, D], F32R)
        q_hi = sb("q_hi", [P, 2, S], F32R)
        q_lo = sb("q_lo", [P, 2, S], F32R)
        rope_cos = sb("rope_cos", [P, 2, S])
        rope_rot = sb("rope_rot", [P, 2, S])
        vT = sb("vT", [P, S])
        prob = sb("prob", [P, 2, SCOL[4]])
        pT_3 = sb("pT_3", [P, P])
        v_3 = sb("v_3", [P, B, D])
        k_0 = sb("k_0", [P, B, P])
        pT_hi = sb("pT_hi", [P, PT_END], F32R)
        pT_lo = sb("pT_lo", [P, PT_END], F32R)
        ctx_hi = sb("ctx_hi", [P, B, R, S], F32R)
        ctx_lo = sb("ctx_lo", [P, B, R, S], F32R)
        cos_sb = sb("cos_sb", [P, S])
        sin_sb = sb("sin_sb", [P, S])
        mask_sb = sb("mask_sb", [P, S])
        ident = sb("ident", [P, P])
        bias_rows = sb("bias_rows", [H + 2 * G, D])
        bias_cols = sb("bias_cols", [P, H + 2 * G])
        row_bias = sb("row_bias", [P, HID])
        negmax = sb("negmax", [P, 2, TT])
        rowsum = sb("rowsum", [P, 2, TT])
        rinv = sb("rinv", [P, 2, TT])
        ids_sb = sb("ids_sb", [P, E])
        act_i = sb("act_i", [P, N_ACTIVE], I32)
        act_f = sb("act_f", [P, 3, N_ACTIVE])
        cnt = sb("cnt", [P, N_ACTIVE + 1, E])
        prior_sb = sb("prior_sb", [P, E])
        rb_sb = sb("rb_sb", [P, E])
        logit_c = sb("logit_c", [P, 4, E])
        neg_half = sb("neg_half", [P, TT])
        ln1_stats = sb("ln1_stats", [P, TT, 6])
        ln1_mv = sb("ln1_mv", [P, TT, 2])
        ln1_tmp = sb("ln1_tmp", [P, 6, TT])
        lnst = sb("lnst", [P, 2, 16])
        sms = sb("sms", [P, 3, TT])
        wb_raw, la_raw, lb_raw = wq_raw, wk_raw, wv_raw
        wbT_hi = wq_hi[:].rearrange("p r k d -> p r (k d)")
        wbT_lo = wq_lo[:].rearrange("p r k d -> p r (k d)")
        ar_hi = wkv_hi[:].rearrange("p a k d -> p (a k d)").rearrange("p (k c) -> p k c", c=ARW)
        ar_lo = wkv_lo[:].rearrange("p a k d -> p (a k d)").rearrange("p (k c) -> p k c", c=ARW)
        lbT_hi, lbT_lo = k_hi[:, 0, :], k_lo[:, 0, :]
        lb_jer = vT
        rt_raw = wo_raw[0:E, 0, :]
        zz = rope_rot
        zT_hi, zT_lo = q_hi, q_lo
        sm = rope_cos[:, 0, 0:4 * TT * E].rearrange("p (s t e) -> p s t e", s=4, t=TT)

        ps_proj = [ps("ps_proj0"), ps("ps_proj1")]
        ps_sc = [ps("ps_sc0"), ps("ps_sc1")]
        ps_tr = [ps("ps_tr0"), ps("ps_tr1")]
        ps_ctx = ps("ps_ctx")
        ps_out = ps("ps_out")
        ps_x = [*ps_tr, *ps_sc, ps_ctx, ps_out, ps_ctx, ps_out]
        ps_y = [ps_sc[0], ps_sc[1], ps_out, ps_ctx]

        x_in = [sem(f"x_in{i}") for i in range(TT)] + [sem("x_in_b1")]
        x_tr, x_hi_d, x_lo_d = sem("x_tr"), sem("x_hi_d"), sem("x_lo_d")
        ident_in, bias_in, rope_in, mask_in = sem("ident_in"), sem("bias_in"), sem("rope_in"), sem("mask_in")
        bo_in, prior_in, small_in = sem("bo_in"), sem("prior_in"), sem("small_in")
        wq_in, wk_in, wv_in, wo_in = [sem("wq_in0"), sem("wq_in1")], sem("wk_in"), sem("wv_in"), sem("wo_in")
        wb_in, la_in, lb_in, rt_in, bb_in = sem("wb_in"), sem("la_in"), sem("lb_in"), sem("rt_in"), sem("bb_in")
        out_done = sem("out_done")
        bias_tr, bias_done, acc_init = sem("bias_tr"), sem("bias_done"), sem("acc_init")
        const_done = sem("const_done")
        wq_hi_d, wq_lo_d = sem("wq_hi_d"), sem("wq_lo_d")
        wk_hi_d, wk_lo_d = sem("wk_hi_d"), sem("wk_lo_d")
        wv_hi_d, wv_lo_d = sem("wv_hi_d"), sem("wv_lo_d")
        wo_hi_d, wo_lo_d = sem("wo_hi_d"), sem("wo_lo_d")
        proj_done, evac_done = sem("proj_done"), sem("evac_done")
        cos_done, sin_done, rope_done = sem("cos_done"), sem("sin_done"), sem("rope_done")
        qk_hi_d, qk_lo_d = sem("qk_hi_d"), sem("qk_lo_d")
        sc_done, max_done, exp_done = sem("sc_done"), sem("max_done"), sem("exp_done")
        rinv_done, p_ready = sem("rinv_done"), sem("p_ready")
        tr_done, tr_hi_d, tr_lo_d = sem("tr_done"), sem("tr_hi_d"), sem("tr_lo_d")
        pv_done, ctx_hi_d, ctx_lo_d = sem("pv_done"), sem("ctx_hi_d"), sem("ctx_lo_d")
        wo_done, acc_done = sem("wo_done"), sem("acc_done")
        dve_chain, ln_done = sem("dve_chain"), sem("ln_done")
        stats_done, pool_chain, ve_done, rstd_done, x1b_done = sem("stats_done"), sem("pool_chain"), sem("ve_done"), sem("rstd_done"), sem("x1b_done")
        lb_sorted, pad_done, ln_prior, prior_eps = sem("lb_sorted"), sem("pad_done"), sem("ln_prior"), sem("prior_eps")
        z_done, nmx_done, e_done, zz_done = sem("z_done"), sem("nmx_done"), sem("e_done"), sem("zz_done")
        y_done, y_added, h2_done = sem("y_done"), sem("y_added"), sem("h2_done")
        prep_done, prep_hi_d, prep_lo_d = sem("prep_done"), sem("prep_hi_d"), sem("prep_lo_d")
        late_done, late_hi_d, late_lo_d = sem("late_done"), sem("late_hi_d"), sem("late_lo_d")

        def wait(eng, s, value):
            if isinstance(value, int) and value <= 0:
                return
            eng.wait_ge(s, value)

        def has(g):
            if not isinstance(g, int):
                return True, True, True
            return 1 <= g <= G, 0 <= g < G, g < G - 1

        def first(g):
            return isinstance(g, int) and g < 0

        def three(out_ap, w_hi, w_lo, m_hi, m_lo, first, last):
            nc.tensor.matmul(out_ap, w_hi, m_hi, start=first, stop=False)
            nc.tensor.matmul(out_ap, w_hi, m_lo, start=False, stop=False)
            return nc.tensor.matmul(out_ap, w_lo, m_hi, start=False, stop=last)

        def z_view(i):
            return ps_proj[(i % TT) // 2][:, (i % 2) * ARW:(i % 2 + 1) * ARW]

        def prep_view(k):
            full = ps_proj[k % 2][:]
            if k == PREP_RT:
                return full[:, 0:KT * E].rearrange("p (k c) -> p k c", k=KT)
            if k == PREP_A:
                return full.rearrange("p (k c) -> p k c", k=KT)
            return full.rearrange("p (j q) -> p j q", j=4) if k == PREP_LB else full

        def prep_dst(k, wbT, ar, lbT):
            if k == PREP_RT:
                return ar[:, :, ER:ER + E]
            if k == PREP_A:
                return ar[:, :, 0:ER]
            return lbT.rearrange("p (q j) -> p j q", j=4) if k == PREP_LB else wbT[:, k, :]

        PREP_LATE = (5, 6)

        def preps(g, n, place):
            if not isinstance(g, int) or g != G - 1:
                return ()
            return {(6, 0): (0, 1), (6, 2): (2,), (7, 0): (3,), (7, 1): (4,)}.get((n, place), ())

        block = ctx.enter_context(nc.Block())

        @block.sync
        def _(sp):
            half = R * D // 2

            def wq_half(i, start):
                sp.dma_start(wq_raw[:, :, i * half:(i + 1) * half], wq_v[:, :, start]).then_inc(wq_in[i], 16)
            sp.dma_start(ident[:], ident_t).then_inc(ident_in, 16)
            sp.dma_start(prior_sb[:], prior.partition_broadcast(P)).then_inc(prior_in, 16)
            for i in range(TT):
                sp.dma_start(acc[:, i, :], x_v[:, i, :]).then_inc(x_in[i], 16)
                if i == 0:
                    sp.dma_start(wk_raw[:], wk_v[:, :, 0:D]).then_inc(wk_in, 16)
            sp.dma_start(bias_rows[0:H, :], bq.rearrange("(h d) -> h d", d=D)).then_inc(bias_in, 16)
            sp.dma_start(bias_rows[H:H + G, :], bk.rearrange("(h d) -> h d", d=D)).then_inc(bias_in, 16)
            sp.dma_start(bias_rows[H + G:H + 2 * G, :], bv.rearrange("(h d) -> h d", d=D)).then_inc(bias_in, 16)
            wq_half(0, slice(0, half))
            sp.dma_start(cos_sb[:], cos_t).then_inc(rope_in, 16)
            sp.dma_start(sin_sb[:], sin_t).then_inc(rope_in, 16)
            sp.dma_start(wv_raw[:], wv_v[:, :, 0:D]).then_inc(wv_in, 16)
            sp.dma_start(row_bias[:], bo.partition_broadcast(P)).then_inc(bo_in, 16)
            sp.dma_start(acc[:, TT:NT, :], x_v[:, TT:NT, :]).then_inc(x_in[TT], 16)
            sp.dma_start(mask_sb[:], mask_t).then_inc(mask_in, 16)
            wq_half(1, slice(half, 2 * half))
            sp.dma_start(wo_raw[:], wo_v[:, 0:R, :]).then_inc(wo_in, 16)
            sp.dma_start(rb_sb[:], router_b.partition_broadcast(P)).then_inc(small_in, 16)
            sp.dma_start(act_i[:], active.partition_broadcast(P)).then_inc(small_in, 16)
            sp.dma_start(ids_sb[:], ids_t).then_inc(small_in, 16)
            with sp.Fori(1, G) as g:
                sp.wait_ge(wk_lo_d, g)
                sp.dma_start(wk_raw[:], wk_v[:, :, bass.ds(g * D, D)]).then_inc(wk_in, 16)
                sp.wait_ge(wv_lo_d, g)
                sp.dma_start(wv_raw[:], wv_v[:, :, bass.ds(g * D, D)]).then_inc(wv_in, 16)
                sp.wait_ge(wq_lo_d, g * R)
                wq_half(0, bass.ds(g * (R * D), half))
                wq_half(1, bass.ds(g * (R * D) + half, half))
                sp.wait_ge(wo_lo_d, g * R)
                sp.dma_start(wo_raw[:], wo_v[:, bass.ds(g * R, R), :]).then_inc(wo_in, 16)
            sp.wait_ge(wq_lo_d, G * R)
            sp.dma_start(wb_raw[:], w_base.rearrange("(t p) h -> p t h", p=P)).then_inc(wb_in, 16)
            sp.wait_ge(wk_lo_d, G)
            sp.dma_start(la_raw[:].rearrange("p k d -> p (k d)"), lora_a.rearrange("e r h -> (e r) h")).then_inc(la_in, 16)
            sp.wait_ge(wv_lo_d, G)
            sp.dma_start(lb_raw[:].rearrange("p k d -> p (k d)").rearrange("p (e c) -> p e c", e=E),
                         lora_b.rearrange("e (p j) r -> p e (j r)", j=4)).then_inc(lb_in, 16)
            sp.wait_ge(wo_lo_d, G * R)
            sp.dma_start(rt_raw, router_w).then_inc(rt_in, 16)
            sp.wait_ge(acc_init, NT)
            sp.dma_start(row_bias[:], b_base.partition_broadcast(P)).then_inc(bb_in, 16)
            for i in range(NT):
                sp.wait_ge(h2_done, i + 1)
                sp.dma_start(out_v[:, i, :], acc[:, i, :]).then_inc(out_done, 16)
            sp.wait_ge(out_done, 16 * NT)

        @block.scalar
        def _(act):
            act.wait_ge(prior_eps, 1)
            act.activation(logit_c[:, 1, :], logit_c[:, 0, :], ACT.Ln).then_inc(ln_prior, 1)
            act.wait_ge(const_done, 1)
            act.activation(sms[:, 0, :], neg_half[:], ACT.Exp)

            def x_high(i):
                act.wait_ge(x_tr, i + 1)
                act.activation(xT_hi[:, :, i * P:(i + 1) * P], ps_x[i][:].rearrange("p (k t) -> p k t", k=KT),
                               ACT.Copy).then_inc(x_hi_d, 1)

            def wq_high(g, h):
                wait(act, wq_in[h // 2], 16 * g + 16)
                act.activation(wq_hi[:, h, :, :], wq_raw[:, :, h * D:(h + 1) * D], ACT.Copy).then_inc(wq_hi_d, 1)

            def wk_high(g):
                wait(act, wk_in, 16 * g + 16)
                act.activation(wkv_hi[:, 0, :, :], wk_raw[:], ACT.Copy).then_inc(wk_hi_d, 1)

            def wv_high(g):
                wait(act, wv_in, 16 * g + 16)
                act.activation(wkv_hi[:, 1, :, :], wv_raw[:], ACT.Copy).then_inc(wv_hi_d, 1)

            x_high(0)
            wk_high(0)
            x_high(1)
            x_high(2)
            x_high(3)
            act.wait_ge(bias_tr, 1)
            act.activation(bias_cols[:], ps_out[:, 0:H + 2 * G], ACT.Copy).then_inc(bias_done, 1)
            wq_high(0, 0)
            wv_high(0)
            wq_high(0, 1)
            act.wait_ge(bias_done, 1)

            projs_due = act.alloc_register("projs_due")

            def projected(proj):
                if isinstance(proj, int):
                    wait(act, proj_done, proj + 1)
                else:
                    act.wait_ge(proj_done, projs_due)
                    act.reg_add(projs_due, projs_due, 1)

            def rotate(proj, rope, bank, slot, col):
                wait(act, rope_done, rope - 1)
                projected(proj)
                h = D // 2
                act.activation(rope_rot[0:h, slot, :], ps_proj[bank][h:D, :], ACT.Identity,
                               bias=bias_cols[h:D, bass.ds(col, 1)])
                act.activation(rope_rot[h:D, slot, :], ps_proj[bank][0:h, :], ACT.Identity,
                               bias=bias_cols[0:h, bass.ds(col, 1)]).then_inc(evac_done, 1)

            def k_high(g, n):
                b, r = (1, rope_k(g, 0)) if n == 1 else (0, rope_k(g, 4))
                sl = rope_slot(ROPE_K[n - 1] + kv_shift(g, n - 1))
                wait(act, rope_done, r + 1)
                wait(act, sc_done, g * (STEPS * SC_PER) + (0 if n == 1 else R * SC_PER))
                act.activation(k_0[:, b, :], rope_cos[:, sl, 0:P], ACT.Copy)
                act.activation(k_hi[:, b, :], rope_cos[:, sl, :], ACT.Copy).then_inc(qk_hi_d, 1)

            def q_high(g, n):
                wait(act, rope_done, rope_q(g, n) + 1)
                wait(act, sc_done, (g * STEPS + n + 1) * SC_PER)
                act.activation(q_hi[:, n % 2, :], rope_cos[:, rope_slot(ROPE_Q[n] + q_shift(g, n)), :], ACT.Copy).then_inc(qk_hi_d, 1)

            def prep_hi(k):
                wait(act, prep_done, k + 1)
                act.activation(prep_dst(k, wbT_hi, ar_hi, lbT_hi), prep_view(k), ACT.Copy).then_inc(prep_hi_d, 1)

            def step(g, n):
                prev, cur, nxt = has(g)
                if (cur if n else prev):
                    N, m = g * STEPS + (n - 1), (n - 1) % STEPS
                    b, h = m // R, m % R
                    wait(act, pv_done, N + 1)
                    if h == 0:
                        wait(act, wo_done, g * STEPS - (STEPS - TT) if b == 0 else g * STEPS)
                    act.activation(ctx_hi[:, b, h, :], ps_ctx[:], ACT.Copy).then_inc(ctx_hi_d, 1)
                if cur:
                    N, t = g * STEPS + n, tr_no(g, TR_P[n])
                    wait(act, pv_done, N)
                    wait(act, tr_done, t + 1)
                    act.activation(pT_3[:], ps_tr[(1 + TR_P[n]) % 2][:, 0:P], ACT.Copy)
                    act.activation(pT_hi[:, PT_T1:PT_T0], ps_tr[(1 + TR_P[n]) % 2][:, P:S], ACT.Copy).then_inc(tr_hi_d, 1)
                    wait(act, tr_done, t + 2)
                    act.activation(pT_hi[:, PT_T0:PT_T2], ps_tr[TR_P[n] % 2][:], ACT.Copy).then_inc(tr_hi_d, 1)
                if isinstance(g, int) and g == 0 and n == 0:
                    q_high(-1, 7)
                    x_high(TT + 2)
                    x_high(TT + 3)
                has_q = cur if n < 6 else nxt
                if has_q:
                    m = (n + 2) % STEPS
                    col = g * R + m % R if n < 6 else g * R + (R + m % R)
                    rotate(proj_q(g, n), rope_q(g, n), bank_q(g, n), rope_slot(ROPE_Q[n] + q_shift(g, n)), col)
                if first(g) and n == 6:
                    k_high(g, 5)
                for k in preps(g, n, 0):
                    prep_hi(k)
                if cur:
                    wait(act, tr_done, t + 3)
                    act.activation(pT_hi[:, PT_T2:PT_END], ps_tr[(1 + TR_P[n]) % 2][:, 0:256], ACT.Copy).then_inc(tr_hi_d, 1)
                has_s = cur if n < 7 else nxt
                slot = (n + 1) % 2

                def exps(i):
                    return act.activation(prob[:, slot, SCOL[i]:SCOL[i + 1]], prob[:, slot, SCOL[i]:SCOL[i + 1]],
                                          ACT.Exp, bias=negmax[:, slot, i:i + 1], scale=-1.0,
                                          accum_out=rowsum[:, slot, i:i + 1])
                V0 = (g * STEPS + n + 1) * SC_PER
                if has_s:
                    wait(act, max_done, V0 + 1)
                    exps(1)
                    exps(0)
                    wait(act, max_done, V0 + 2)
                    exps(2).then_inc(exp_done, 1)
                    wait(act, max_done, V0 + 3)
                    exps(3).then_inc(exp_done, 1)
                for k in (*preps(g, n, 1), *preps(g, n, 2)):
                    prep_hi(k)
                if n in (0, 4) and (cur if n == 0 else nxt):
                    col = g + H if n == 0 else g + (H + 1)
                    rotate(proj_kv(g, n), rope_k(g, n), bank_kv(g, n), rope_slot(ROPE_K[n] + kv_shift(g, n)), col)
                if first(g) and n == 6:
                    q_high(g, n)
                if n in (2, 6) and (cur if n == 2 else nxt):
                    wait(act, tr_done, (tr_no(g, TR_V[3]) if n == 6 else tr_no(g - 1, TR_V[7])) + 1)
                    projected(proj_kv(g, n))
                    col = g + (H + G) if n == 2 else g + (H + G + 1)
                    act.activation(vT[:], ps_proj[bank_kv(g, n)][:], ACT.Identity,
                                   bias=bias_cols[:, bass.ds(col, 1)]).then_inc(evac_done, 1)
                if ((n == 1 and cur) or (n == 5 and nxt)) and not first(g):
                    k_high(g, n)
                if has_q and not first(g):
                    q_high(g, n)
                if first(g) and n == 6:
                    x_high(TT)
                    x_high(TT + 1)
                    wq_high(0, 2)
                if n in TR_V and (cur if n == 3 else nxt):
                    b = 1 if n == 3 else 0
                    wait(act, tr_done, tr_no(g, TR_V[n]) + 1)
                    wait(act, pv_done, g * STEPS + (0 if n == 3 else R))
                    act.activation(v_3[:, b, :], ps_tr[(1 + TR_V[n]) % 2][:, S - P:S], ACT.Copy)
                    act.activation(v_hi[:, b, :, :], ps_tr[(1 + TR_V[n]) % 2][:].rearrange("p (t d) -> p t d", t=TT),
                                   ACT.Copy).then_inc(tr_hi_d, 1)
                if first(g) and n == 7:
                    wq_high(0, 3)
                if cur and n == 3:
                    wait(act, wo_in, 16 * g + 16)
                    wait(act, wo_done, STEPS * g)
                    for h in range(R):
                        act.activation(wo_hi[:, h, :], wo_raw[:, h, :], ACT.Copy).then_inc(wo_hi_d, 1)
                if nxt and not first(g):
                    if n == 2:
                        wait(act, proj_done, proj_kv(g, 0) + 1)
                        wk_high(g + 1)
                    if n >= 4:
                        h = n - 4
                        wait(act, proj_done, proj_q(g, h + 2) + 1)
                        wq_high(g + 1, h)
                    if n == 5:
                        wait(act, proj_done, proj_kv(g, 2) + 1)
                        wv_high(g + 1)

            for g in (-1, 0):
                for n in range(STEPS):
                    step(g, n)
            act.reg_mov(projs_due, proj_q(1, 0) + 1)
            with act.Fori(1, G - 1) as g:
                for n in range(STEPS):
                    step(g, n)
            for n in range(STEPS):
                step(G - 1, n)
            step(G, 0)
            for k in PREP_LATE:
                prep_hi(k)

            def x1T_hi(i):
                act.wait_ge(late_done, i + 1)
                act.activation(xT_hi[:, :, i * P:(i + 1) * P], ps_tr[i % 2][:].rearrange("p (k t) -> p k t", k=KT),
                               ACT.Copy).then_inc(late_hi_d, 1)

            def zT_high(b):
                act.wait_ge(late_done, LATE_Z + b + 1)
                act.activation(zT_hi[:, b, :], ps_tr[b][:], ACT.Copy).then_inc(late_hi_d, 1)

            def router_exps(b):
                act.wait_ge(nmx_done, b + 1)
                for t in range(TT):
                    last = act.activation(sm[:, 1, t, :], sm[:, 0, t, :], ACT.Exp, bias=sms[:, 0, t:t + 1], scale=-1.0)
                last.then_inc(e_done, 1)
            for i in range(TT):
                x1T_hi(i)
            router_exps(0)
            for i in range(TT, NT):
                x1T_hi(i)
            zT_high(0)
            router_exps(1)
            zT_high(1)

        @block.gpsimd
        def _(pool):
            pool.memset(neg_half[:], -0.5).then_inc(const_done, 1)

            def low(dst, full, high):
                return pool.tensor_tensor(dst, full, high.bitcast(F32), ALU.subtract)

            def wq_low(g, h):
                wait(pool, wq_hi_d, g * R + h + 1)
                low(wq_lo[:, h, :, :], wq_raw[:, :, h * D:(h + 1) * D], wq_hi[:, h, :, :]).then_inc(wq_lo_d, 1)

            def wk_low(g):
                wait(pool, wk_hi_d, g + 1)
                low(wkv_lo[:, 0, :, :], wk_raw[:], wkv_hi[:, 0, :, :]).then_inc(wk_lo_d, 1)

            def wv_low(g):
                wait(pool, wv_hi_d, g + 1)
                low(wkv_lo[:, 1, :, :], wv_raw[:], wkv_hi[:, 1, :, :]).then_inc(wv_lo_d, 1)

            def init_acc(i):
                pool.wait_ge(x_tr, i + 1)
                pool.tensor_tensor(acc[:, i, :], acc[:, i, :], row_bias[:], ALU.add).then_inc(acc_init, 1)

            def sine(proj, r, slot):
                wait(pool, evac_done, proj + 1)
                pool.tensor_tensor(rope_rot[:, slot, :], rope_rot[:, slot, :], sin_sb[:], ALU.mult).then_inc(sin_done, 1)

            def step(g, n):
                prev, cur, nxt = has(g)
                has_k = (n == 1 and cur) or (n == 5 and nxt)
                if has_k:
                    r = rope_k(g, n - 1)
                    sl = rope_slot(ROPE_K[n - 1] + kv_shift(g, n - 1))
                    if not first(g):
                        sine(proj_kv(g, n - 1), r, sl)
                has_q = cur if n < 6 else nxt
                if has_q and not first(g):
                    sine(proj_q(g, n), rope_q(g, n), rope_slot(ROPE_Q[n] + q_shift(g, n)))
                if has_k:
                    b = 1 if n == 1 else 0
                    wait(pool, qk_hi_d, r + 1)
                    low(k_lo[:, b, :], rope_cos[:, sl, :], k_hi[:, b, :]).then_inc(qk_lo_d, 1)
                if has_q:
                    wait(pool, qk_hi_d, rope_q(g, n) + 1)
                    low(q_lo[:, n % 2, :], rope_cos[:, rope_slot(ROPE_Q[n] + q_shift(g, n)), :],
                        q_hi[:, n % 2, :]).then_inc(qk_lo_d, 1)
                if cur and n == 3:
                    for h in range(R):
                        wait(pool, wo_hi_d, g * R + h + 1)
                        low(wo_lo[:, h, :], wo_raw[:, h, :], wo_hi[:, h, :]).then_inc(wo_lo_d, 1)
                if nxt and not first(g):
                    if n == 2:
                        wk_low(g + 1)
                    if n >= 4:
                        wq_low(g + 1, n - 4)
                    if n == 5:
                        wv_low(g + 1)
                if first(g) and n == 6:
                    wq_low(0, 2)
                    init_acc(2)
                    wq_low(0, 3)
                    init_acc(3)
                if isinstance(g, int) and g == 0 and n >= TT:
                    init_acc(n)
                if isinstance(g, int) and g == G - 1 and n == 5:
                    pool.wait_ge(proj_done, proj_kv(g, 2) + 1)
                    pool.memset(ar_hi[:, :, ER + E:ARW].bitcast(F32), 0.0)
                    pool.memset(ar_lo[:, :, ER + E:ARW].bitcast(F32), 0.0).then_inc(pad_done, 1)
                    pool.wait_ge(lb_in, 16)
                    pool.wait_ge(tr_done, tr_no(g, TR_V[3]) + 1)
                    pool.tensor_copy(lb_jer[:].rearrange("p (j e r) -> p e j r", j=4, e=E),
                                     lb_raw[:].rearrange("p k d -> p (k d)").rearrange("p (e j r) -> p e j r", e=E, j=4)
                                     ).then_inc(lb_sorted, 1)

            wk_low(0)
            wq_low(0, 0)
            wv_low(0)
            wq_low(0, 1)
            pool.wait_ge(bo_in, 16)
            init_acc(0)
            init_acc(1)
            pool.wait_ge(rope_in, 32)
            for n in range(STEPS):
                step(-1, n)
            for n in range(STEPS):
                step(0, n)
            with pool.Fori(1, G - 1) as g:
                for n in range(STEPS):
                    step(g, n)
            for n in range(STEPS):
                step(G - 1, n)

            pool.wait_ge(bb_in, 16)
            pool.wait_ge(const_done, 1)

            def rstd(c, dst, var, tmp):
                pool.wait_ge(ve_done, c + 1)
                y, t0, t1, t2 = (tmp(j) for j in range(4))
                own = (c * 4 + 1, c * 4 + 2, c * 4 + 3, c * 4 + 4)
                pool.tensor_tensor(y, var, neg_half[:, 0:var.shape[-1]], ALU.pow).then_inc(pool_chain, 1)
                pool.wait_ge(pool_chain, own[0])
                pool.tensor_tensor(t0, var, y, ALU.mult).then_inc(pool_chain, 1)
                pool.wait_ge(pool_chain, own[1])
                pool.tensor_tensor(t1, t0, y, ALU.mult).then_inc(pool_chain, 1)
                pool.wait_ge(pool_chain, own[2])
                pool.tensor_scalar(t2, t1, -0.5, 1.5, ALU.mult, ALU.add).then_inc(pool_chain, 1)
                pool.wait_ge(pool_chain, own[3])
                pool.tensor_tensor(dst, t2, y, ALU.mult).then_inc(rstd_done, 1)
            for b in range(B):
                rstd(b, ln1_tmp[:, 5, :], ln1_tmp[:, 0, :], lambda j: ln1_tmp[:, 1 + j, :])
                for i in range(b * TT, (b + 1) * TT):
                    pool.wait_ge(late_done, i + 1)
                    pool.tensor_tensor(acc[:, i, :], acc[:, i, :], row_bias[:], ALU.add).then_inc(x1b_done, 1)
            for i in range(NT):
                rstd(B + i, lnst[:, i % 2, 13:14], lnst[:, i % 2, 8:9], lambda j: lnst[:, i % 2, 9 + j:10 + j])

        @block.vector
        def _(dve):
            chain = [0]

            def link(ins):
                chain[0] += 1
                ins.then_inc(dve_chain, 1)
                dve.wait_ge(dve_chain, chain[0])

            dve.wait_ge(prior_in, 16)
            nc.vector.tensor_scalar(logit_c[:, 0, :], prior_sb[:], PRIOR_EPS, None, ALU.add).then_inc(prior_eps, 1)

            def router_constants():
                dve.wait_ge(small_in, 48)
                link(nc.vector.tensor_copy(act_f[:, 0, :], act_i[:]))
                link(nc.vector.tensor_scalar(act_f[:, 1, :], act_f[:, 0, :], 0.0, float(E), ALU.is_lt, ALU.mult))
                link(nc.vector.tensor_tensor(act_f[:, 2, :], act_f[:, 0, :], act_f[:, 1, :], ALU.add))
                link(nc.vector.tensor_scalar(cnt[:, 0, :], ids_sb[:], act_f[:, 2, 0:1], None, ALU.is_equal))
                for a in range(1, N_ACTIVE):
                    link(nc.vector.scalar_tensor_tensor(cnt[:, a, :], ids_sb[:], act_f[:, 2, a:a + 1], cnt[:, a - 1, :],
                                                        ALU.is_equal, ALU.add))
                link(nc.vector.tensor_scalar(cnt[:, N_ACTIVE, :], cnt[:, N_ACTIVE - 1, :], 0.0, OFF, ALU.is_equal, ALU.mult))
                dve.wait_ge(ln_prior, 1)
                link(nc.vector.tensor_tensor(logit_c[:, 2, :], logit_c[:, 1, :], rb_sb[:], ALU.add))
                link(nc.vector.tensor_tensor(logit_c[:, 3, :], logit_c[:, 2, :], cnt[:, N_ACTIVE, :], ALU.add))

            def low(dst, full, high):
                return nc.vector.tensor_tensor(dst, full, high.bitcast(F32), ALU.subtract)

            def x_low(i):
                dve.wait_ge(x_hi_d, i + 1)
                cols = slice(i * P, (i + 1) * P)
                low(xT_lo[:, :, cols], ps_x[i][:].rearrange("p (k t) -> p k t", k=KT), xT_hi[:, :, cols]).then_inc(x_lo_d, 1)
            for i in range(TT):
                x_low(i)
            dve.wait_ge(bias_done, 1)
            dve.wait_ge(rope_in, 32)

            tiles_seen = dve.alloc_register("score_tiles")

            def rope_part1(proj, r, bank, slot, col):
                wait(dve, qk_lo_d, r - 1)
                wait(dve, evac_done, proj + 1)
                nc.vector.scalar_tensor_tensor(rope_cos[:, slot, :], ps_proj[bank][:], bias_cols[:, bass.ds(col, 1)],
                                               cos_sb[:], ALU.add, ALU.mult).then_inc(cos_done, 1)

            def rope_part2(r, slot):
                if isinstance(r, int) and r < N_FIRST:
                    link(nc.vector.tensor_tensor(rope_rot[:, slot, :], rope_rot[:, slot, :], sin_sb[:], ALU.mult))
                else:
                    wait(dve, sin_done, r + 1 - N_FIRST)
                wait(dve, cos_done, r + 1)
                nc.vector.tensor_tensor(rope_cos[:, slot, :], rope_cos[:, slot, :], rope_rot[:, slot, :],
                                        ALU.add).then_inc(rope_done, 1)

            def step(g, n):
                prev, cur, nxt = has(g)
                N = g * STEPS + n
                early_add = isinstance(g, int) and N >= STEPS * G - 2
                if early_add:
                    add_previous(g, n)
                if (cur if n else prev):
                    m = (n - 1) % STEPS
                    wait(dve, ctx_hi_d, N)
                    low(ctx_lo[:, m // R, m % R, :], ps_ctx[:], ctx_hi[:, m // R, m % R, :]).then_inc(ctx_lo_d, 1)
                if cur:
                    t = tr_no(g, TR_P[n])
                    wait(dve, tr_hi_d, t + 1)
                    low(pT_lo[:, PT_T1:PT_T0], ps_tr[(1 + TR_P[n]) % 2][:, P:S], pT_hi[:, PT_T1:PT_T0]).then_inc(tr_lo_d, 1)
                    wait(dve, tr_hi_d, t + 2)
                    low(pT_lo[:, PT_T0:PT_T2], ps_tr[TR_P[n] % 2][:], pT_hi[:, PT_T0:PT_T2]).then_inc(tr_lo_d, 1)
                has_k = (n == 1 and cur) or (n == 5 and nxt)
                if has_k:
                    k_slot = rope_slot(ROPE_K[n - 1] + kv_shift(g, n - 1))
                    col = g + H if n == 1 else g + (H + 1)
                    rope_part1(proj_kv(g, n - 1), rope_k(g, n - 1), bank_kv(g, n - 1), k_slot, col)
                if not early_add:
                    add_previous(g, n)
                if isinstance(g, int) and g == 0 and n == 0:
                    x_low(TT + 2)
                    x_low(TT + 3)
                if has_k:
                    rope_part2(rope_k(g, n - 1), k_slot)
                slot = (n + 1) % 2
                has_s = cur if n < 7 else nxt

                def masked(i, bank, at):
                    w = (i + 1) * P
                    return nc.vector.tensor_tensor_reduce(
                        out=prob[:, slot, SCOL[i]:SCOL[i + 1]], in0=ps_sc[bank][:, at:at + w], in1=mask_sb[:, S - w:S],
                        scale=-SCALE, scalar=BIG, op0=ALU.add, op1=ALU.min, accum_out=negmax[:, slot, i:i + 1])

                def tile_ready(v):
                    if isinstance(g, int):
                        wait(dve, sc_done, (N + 1) * SC_PER + v + 1)
                    else:
                        dve.wait_ge(sc_done, tiles_seen)
                        dve.reg_add(tiles_seen, tiles_seen, 1)
                if first(g) and n == 7:
                    dve.wait_ge(mask_in, 16)
                if has_s:
                    tile_ready(0)
                    masked(1, (n + 1) % 2, 0)
                    masked(0, (n + 1) % 2, 256).then_inc(max_done, 1)
                    tile_ready(1)
                    masked(2, n % 2, 0).then_inc(max_done, 1)
                has_q = cur if n < 6 else nxt
                m = (n + 2) % STEPS
                col = g * R + m % R if n < 6 else g * R + (R + m % R)
                q_slot = rope_slot(ROPE_Q[n] + q_shift(g, n))
                late_q = first(g) and n == 7
                if has_q and not late_q:
                    rope_part1(proj_q(g, n), rope_q(g, n), bank_q(g, n), q_slot, col)
                for k in preps(g, n, 0):
                    prep_lo(k)
                if cur:
                    wait(dve, tr_hi_d, t + 3)
                    low(pT_lo[:, PT_T2:PT_END], ps_tr[(1 + TR_P[n]) % 2][:, 0:256], pT_hi[:, PT_T2:PT_END]).then_inc(tr_lo_d, 1)
                if has_s:
                    tile_ready(2)
                    masked(3, (n + 1) % 2, 0).then_inc(max_done, 1)
                if has_q and not late_q:
                    rope_part2(rope_q(g, n), q_slot)
                if has_s:
                    for part, (i0, i1) in enumerate(((0, TT - 1), (TT - 1, TT))):
                        wait(dve, exp_done, 2 * N + 3 + part)
                        nc.vector.reciprocal(rinv[:, slot, i0:i1], rowsum[:, slot, i0:i1]).then_inc(rinv_done, 1)
                        wait(dve, rinv_done, 2 * N + 3 + part)
                        for i in range(i0, i1):
                            last = nc.vector.tensor_scalar(prob[:, slot, SCOL[i]:SCOL[i + 1]],
                                                           prob[:, slot, SCOL[i]:SCOL[i + 1]],
                                                           rinv[:, slot, i:i + 1], None, ALU.mult)
                    last.then_inc(p_ready, 1)
                for k in (*preps(g, n, 1), *preps(g, n, 2)):
                    prep_lo(k)
                if first(g) and n == 6:
                    x_low(TT)
                    x_low(TT + 1)
                if isinstance(g, int) and g == G - 1 and n == 7:
                    router_constants()
                if n in TR_V and (cur if n == 3 else nxt):
                    b = 1 if n == 3 else 0
                    wait(dve, tr_hi_d, tr_no(g, TR_V[n]) + 1)
                    low(v_lo[:, b, :, :], ps_tr[(1 + TR_V[n]) % 2][:].rearrange("p (t d) -> p t d", t=TT),
                        v_hi[:, b, :, :]).then_inc(tr_lo_d, 1)
                if late_q:
                    rope_part1(proj_q(g, n), rope_q(g, n), bank_q(g, n), q_slot, col)
                    rope_part2(rope_q(g, n), q_slot)

            def add_previous(g, n):
                prev, cur, nxt = has(g)
                if (prev if n <= R else cur):
                    add_tile(g * STEPS + (n - R - 1), (n - R - 1) % STEPS)
                    if isinstance(g, int) and g * STEPS + (n - R - 1) >= STEPS * (G - 1):
                        tile_stats((n - R - 1) % STEPS)

            def prep_lo(k):
                wait(dve, prep_hi_d, k + 1)
                low(prep_dst(k, wbT_lo, ar_lo, lbT_lo), prep_view(k), prep_dst(k, wbT_hi, ar_hi, lbT_hi)).then_inc(prep_lo_d, 1)

            def tile_stats(i):
                dve.wait_ge(acc_done, STEPS * (G - 1) + i + 1)
                nc.vector.bn_stats(ln1_stats[:, i % TT, :], acc[:, i, :]).then_inc(stats_done, 1)

            def add_tile(w, tile, bank=None):
                if isinstance(w, int) and w < NT:
                    wait(dve, acc_init, w + 1)
                wait(dve, wo_done, w + 1)
                nc.vector.tensor_tensor(acc[:, tile, :], acc[:, tile, :], (bank or ps_out)[:], ALU.add).then_inc(acc_done, 1)

            for g in (-1, 0):
                for n in range(STEPS):
                    step(g, n)
            dve.reg_mov(tiles_seen, (STEPS + 1) * SC_PER + 1)
            with dve.Fori(1, G - 1) as g:
                for n in range(STEPS):
                    step(g, n)
            for n in range(STEPS):
                step(G - 1, n)
            step(G, 0)
            for k in PREP_LATE:
                prep_lo(k)

            def first_norm(b):
                dve.wait_ge(stats_done, (b + 1) * TT)
                for t in range(TT):
                    last = nc.vector.bn_aggr(ln1_mv[:, t, :], ln1_stats[:, t, :])
                link(last)
                nc.vector.tensor_scalar(ln1_tmp[:, 0, :], ln1_mv[:, :, 1], LN_EPS, None, ALU.add).then_inc(ve_done, 1)
                dve.wait_ge(rstd_done, b + 1)
                for t in range(TT):
                    i = b * TT + t
                    nc.vector.tensor_scalar(acc[:, i, :], acc[:, i, :], ln1_mv[:, t, 0:1], ln1_tmp[:, 5, t:t + 1],
                                            ALU.subtract, ALU.mult).then_inc(ln_done, 1)

            def x1T_low(i):
                cols = slice(i * P, (i + 1) * P)
                dve.wait_ge(late_hi_d, i + 1)
                low(xT_lo[:, :, cols], ps_tr[i % 2][:].rearrange("p (k t) -> p k t", k=KT), xT_hi[:, :, cols]).then_inc(late_lo_d, 1)

            def zT_low(b):
                dve.wait_ge(late_hi_d, LATE_Z + b + 1)
                low(zT_lo[:, b, :], ps_tr[b][:], zT_hi[:, b, :]).then_inc(late_lo_d, 1)

            def router(b):
                dve.wait_ge(z_done, (b + 1) * TT)
                for t in range(TT):
                    last = nc.vector.tensor_tensor_reduce(out=sm[:, 0, t, :], in0=z_view(t)[:, ER:ER + E], in1=logit_c[:, 3, :],
                                                          scale=-1.0, scalar=BIG, op0=ALU.add, op1=ALU.min,
                                                          accum_out=sms[:, 0, t:t + 1])
                last.then_inc(nmx_done, 1)
                dve.wait_ge(e_done, b + 1)
                for t in range(TT):
                    last = nc.vector.tensor_tensor_reduce(out=sm[:, 2, t, :], in0=sm[:, 1, t, :], in1=cnt[:, N_ACTIVE - 1, :],
                                                          scale=1.0, scalar=0.0, op0=ALU.mult, op1=ALU.add,
                                                          accum_out=sms[:, 1, t:t + 1])
                link(last)
                link(nc.vector.reciprocal(sms[:, 2, :], sms[:, 1, :]))
                for t in range(TT):
                    last = nc.vector.tensor_scalar(sm[:, 3, t, :], sm[:, 2, t, :], sms[:, 2, t:t + 1], LORA_SCALING,
                                                   ALU.mult, ALU.mult)
                link(last)
                for t in range(TT):
                    last = nc.vector.tensor_tensor(zz[:, b, t * ER:(t + 1) * ER].rearrange("p (e r) -> p e r", r=RANK),
                                                   z_view(t)[:, 0:ER].rearrange("p (e r) -> p e r", r=RANK),
                                                   sm[:, 3, t, :].unsqueeze(2).to_broadcast([P, E, RANK]), ALU.mult)
                last.then_inc(zz_done, 1)

            def finish_sum(i):
                st = lnst[:, i % 2, :]
                dve.wait_ge(y_done, i + 1)
                dve.wait_ge(x1b_done, i + 1)
                nc.vector.tensor_tensor(acc[:, i, :], acc[:, i, :], ps_y[i % TT][:], ALU.add).then_inc(y_added, 1)
                dve.wait_ge(y_added, i + 1)
                link(nc.vector.bn_stats(st[:, 0:6], acc[:, i, :]))
                link(nc.vector.bn_aggr(st[:, 6:8], st[:, 0:6]))
                nc.vector.tensor_scalar(st[:, 8:9], st[:, 7:8], LN_EPS, None, ALU.add).then_inc(ve_done, 1)

            def finish_norm(i):
                st = lnst[:, i % 2, :]
                dve.wait_ge(rstd_done, B + i + 1)
                nc.vector.tensor_scalar(acc[:, i, :], acc[:, i, :], st[:, 6:7], st[:, 13:14], ALU.subtract, ALU.mult).then_inc(h2_done, 1)

            def add_late(t):
                add_tile(STEPS * G - R + t, TT + t, ps_y[t])
                tile_stats(TT + t)

            first_norm(0)
            add_late(0)
            add_late(1)
            x1T_low(0)
            x1T_low(1)
            add_late(2)
            x1T_low(2)
            x1T_low(3)
            add_late(3)
            first_norm(1)
            router(0)
            for i in range(TT, NT):
                x1T_low(i)
            zT_low(0)
            router(1)
            finish_sum(0)
            finish_sum(1)
            finish_norm(0)
            for i in range(2, NT):
                finish_sum(i)
                finish_norm(i - 1)
                if i == 2:
                    zT_low(1)
            finish_norm(NT - 1)

        @block.tensor
        def _(pe):
            pe.wait_ge(ident_in, 16)

            def x_transpose(i):
                pe.wait_ge(x_in[min(i, TT)], 16)
                if i == TT + 1:
                    pe.wait_ge(bias_done, 1)
                if i >= TT + 2:
                    pe.wait_ge(x_lo_d, i - 1)
                for k in range(KT):
                    last = nc.tensor.transpose(ps_x[i][:, k * P:(k + 1) * P], acc[:, i, k * P:(k + 1) * P], ident[:])
                last.then_inc(x_tr, 1)
            for i in range(TT):
                x_transpose(i)
            pe.wait_ge(bias_in, 48)
            nc.tensor.transpose(ps_out[:, 0:H + 2 * G], bias_rows[:], ident[0:H + 2 * G, 0:H + 2 * G]).then_inc(bias_tr, 1)

            def project(w_hi, w_lo, b, bank, t0=0, t1=TT):
                cols = slice(b * S + t0 * P, b * S + t1 * P)
                for k in range(KT):
                    last = three(ps_proj[bank][:, t0 * P:t1 * P], w_hi[:, k, :], w_lo[:, k, :], xT_hi[:, k, cols], xT_lo[:, k, cols],
                                 k == 0, k == KT - 1)
                if t1 == TT:
                    last.then_inc(proj_done, 1)

            def tr_free(g, j):
                wait(pe, tr_lo_d, tr_no(g, j) - 1)

            def proj_bank_free(g, j, number):
                wait(pe, evac_done, number - 1)
                wait(pe, cos_done, ropes_before(g, j))

            def project_kv(g, n):
                prev, cur, nxt = has(g)
                if n % 2 == 0 and (cur if n < 4 else nxt):
                    proj_bank_free(g, PROJ_KV[n] + kv_shift(g, n), proj_kv(g, n))
                    if isinstance(g, int) and g == 0 and n == 0:
                        wait(pe, x_lo_d, NT)
                    which = 0 if n in (0, 4) else 1
                    wait(pe, wk_lo_d if which == 0 else wv_lo_d, g + (1 if n < 4 else 2))
                    weights = wkv_hi[:, which, :, :], wkv_lo[:, which, :, :]
                    if first(g) and n == 4:
                        for t in range(0, TT, 2):
                            wait(pe, x_lo_d, t + 2)
                            project(*weights, 0, bank_kv(g, n), t, t + 2)
                    else:
                        project(*weights, 1 if n < 4 else 0, bank_kv(g, n))

            def step(g, n):
                prev, cur, nxt = has(g)
                slot = n % 2

                def p_tile(t, i, at, bank):
                    c = SCOL[i] + t * P
                    return nc.tensor.transpose(ps_tr[bank][:, at:at + P], prob[:, slot, c:c + P], ident[:])
                if cur:
                    j = TR_P[n]
                    tr_free(g, j)
                    wait(pe, p_ready, g * STEPS + (n + 1))
                    p_tile(3, 3, 0, (1 + j) % 2)
                    for i in range(1, TT):
                        last = p_tile(1, i, i * P, (1 + j) % 2)
                    last.then_inc(tr_done, 1)
                    tr_free(g, j + 1)
                    for i in range(TT):
                        last = p_tile(0, i, i * P, j % 2)
                    last.then_inc(tr_done, 1)
                if cur if n < 6 else nxt:
                    m = (n + 2) % STEPS
                    b, h = m // R, m % R
                    proj_bank_free(g, PROJ_Q[n] + q_shift(g, n), proj_q(g, n))
                    if b == 0:
                        wait(pe, wq_lo_d, g * R + (R + h + 1) if n >= 6 else g * R + (h + 1))
                    project(wq_hi[:, h, :, :], wq_lo[:, h, :, :], b, bank_q(g, n))
                if first(g) and n == 6:
                    x_transpose(TT)
                    x_transpose(TT + 1)
                for k in preps(g, n, 0):
                    prep(k)
                early_out = isinstance(g, int) and g == G - 1 and n == 7
                if early_out:
                    out_heads(g, n, 0, R)
                if cur:
                    tr_free(g, j + 2)
                    for i in range(2, TT):
                        last = p_tile(2, i, (i - 2) * P, (1 + j) % 2)
                    last.then_inc(tr_done, 1)
                has_s = cur if n < 7 else nxt
                m = (n + 1) % STEPS
                V0 = (g * STEPS + (n + 1)) * SC_PER

                def scores(i, bank, at):
                    w = P * (i + 1)
                    q = slice(i * P, (i + 1) * P)
                    if i == 0:
                        gq, nq = (g, n - 1) if n else (g - 1, 7)
                        sl = rope_slot(ROPE_Q[nq] + q_shift(gq, nq))
                        return nc.tensor.matmul(ps_sc[bank][:, at:at + w], rope_cos[:, sl, q], k_0[:, m // R, :],
                                                start=True, stop=True)
                    return three(ps_sc[bank][:, at:at + w], q_hi[:, m % 2, q], q_lo[:, m % 2, q],
                                 k_hi[:, m // R, 0:w], k_lo[:, m // R, 0:w], True, True)
                if has_s:
                    if first(g):
                        wait(pe, x_lo_d, TT)
                    wait(pe, qk_lo_d, (rope_q(g, n - 1) if n else rope_q(g - 1, 7)) + 1)
                    wait(pe, max_done, V0 - 1)
                    scores(1, m % 2, 0)
                    scores(0, m % 2, 256).then_inc(sc_done, 1)
                    wait(pe, max_done, V0)
                    scores(2, (m + 1) % 2, 0).then_inc(sc_done, 1)
                for k in preps(g, n, 1):
                    prep(k)
                late_kv = isinstance(g, int) and g == 0 and n < R
                if not late_kv:
                    project_kv(g, n)
                has_out = (prev if n <= 3 else cur) and not early_out
                ahead = 1 if n % 2 or not (cur if n < 4 else nxt) else 0
                if has_out:
                    out_heads(g, n, 0, ahead)
                if has_s:
                    wait(pe, max_done, V0 + 1)
                    scores(3, m % 2, 0).then_inc(sc_done, 1)
                if late_kv:
                    project_kv(g, n)
                if has_out:
                    out_heads(g, n, ahead, R)
                for k in preps(g, n, 2):
                    prep(k)
                if n in TR_V and (cur if n == 3 else nxt):
                    wait(pe, evac_done, proj_kv(g, n - 1) + 1)
                    tr_free(g, TR_V[n])
                    for t in range(TT):
                        last = nc.tensor.transpose(ps_tr[(1 + TR_V[n]) % 2][:, t * P:(t + 1) * P], vT[:, t * P:(t + 1) * P], ident[:])
                    last.then_inc(tr_done, 1)
                if first(g) and n == 7:
                    x_transpose(TT + 2)
                    x_transpose(TT + 3)
                if cur:
                    N, b = g * STEPS + n, n // R
                    wait(pe, ctx_lo_d, N)
                    wait(pe, tr_lo_d, tr_no(g, TR_P[n]) + 3)
                    for t, c in ((0, PT_T0), (1, PT_T1), (2, PT_T2)):
                        w = S - t * P
                        three(ps_ctx[:, t * P:S], v_hi[:, b, t, :], v_lo[:, b, t, :], pT_hi[:, c:c + w], pT_lo[:, c:c + w],
                              t == 0, False)
                    nc.tensor.matmul(ps_ctx[:, S - P:S], v_3[:, b, :], pT_3[:], start=False, stop=True).then_inc(pv_done, 1)

            def out_heads(g, n, h0, h1, bank=None):
                w, m = g * STEPS + (n - R), (n - R) % STEPS
                b, t = m // TT, m % TT
                if h0 == 0 and h1 > 0 and bank is None:
                    wait(pe, acc_done, w)
                for h in range(h0, h1):
                    if t == 0:
                        wait(pe, ctx_lo_d, g * STEPS + (h + 1 if b == 0 else h + 1 - R))
                    if m == 0:
                        wait(pe, wo_lo_d, g * R + (h + 1))
                    c = slice(t * P, (t + 1) * P)
                    last = three((bank or ps_out)[:], ctx_hi[:, b, h, c], ctx_lo[:, b, h, c], wo_hi[:, h, :], wo_lo[:, h, :],
                                 h == 0, h == R - 1)
                if h1 == R:
                    last.then_inc(wo_done, 1)

            def prep(k):
                if k < 2:
                    wait(pe, evac_done, PROJ_ALL)
                    wait(pe, cos_done, ROPE_ALL)
                wait(pe, prep_lo_d, k - 1)
                bank = ps_proj[k % 2]
                if k < KT:
                    wait(pe, wb_in, 16)
                    for t in range(HID // P):
                        last = nc.tensor.transpose(bank[:, t * P:(t + 1) * P], wb_raw[:, t, k * P:(k + 1) * P], ident[:])
                elif k == PREP_A:
                    wait(pe, la_in, 16)
                    for k2 in range(KT):
                        last = nc.tensor.transpose(bank[:, k2 * P:(k2 + 1) * P], la_raw[:, k2, :], ident[:])
                elif k == PREP_RT:
                    wait(pe, rt_in, 16)
                    for k2 in range(KT):
                        last = nc.tensor.transpose(bank[:, k2 * E:(k2 + 1) * E], rt_raw[:, k2 * P:(k2 + 1) * P], ident[0:E, 0:E])
                else:
                    wait(pe, lb_sorted, 1)
                    for j in range(4):
                        last = nc.tensor.transpose(bank[:, j * P:(j + 1) * P], lb_jer[:, j * ER:(j + 1) * ER], ident[:])
                last.then_inc(prep_done, 1)

            for n in range(STEPS):
                step(-1, n)
            for n in range(STEPS):
                step(0, n)
            with pe.Fori(1, G - 1) as g:
                for n in range(STEPS):
                    step(g, n)
            for n in range(STEPS):
                step(G - 1, n)

            def x1_transpose(i):
                wait(pe, ln_done, i + 1)
                if i < 2:
                    wait(pe, tr_lo_d, TR_ALL)
                wait(pe, late_lo_d, i - 1)
                for k in range(KT):
                    last = nc.tensor.transpose(ps_tr[i % 2][:, k * P:(k + 1) * P], acc[:, i, k * P:(k + 1) * P], ident[:])
                last.then_inc(late_done, 1)

            def out_late(t):
                if t == 0:
                    wait(pe, max_done, STEPS * G * SC_PER)
                if t == 2:
                    wait(pe, acc_done, STEPS * G - R)
                if t == 3:
                    wait(pe, ctx_lo_d, STEPS * G)
                out_heads(G, t, 0, R - 1, ps_y[t])
                if t == 0:
                    for k in PREP_LATE:
                        prep(k)
                out_heads(G, t, R - 1, R, ps_y[t])

            def z_and_logits(i):
                if i == 0:
                    wait(pe, pad_done, 1)
                    wait(pe, prep_lo_d, N_PREP)
                if i == TT:
                    wait(pe, zz_done, 1)
                wait(pe, late_lo_d, i + 1)
                c = slice(i * P, (i + 1) * P)
                for k in range(KT):
                    last = three(z_view(i), xT_hi[:, k, c], xT_lo[:, k, c], ar_hi[:, k, :], ar_lo[:, k, :], k == 0, k == KT - 1)
                last.then_inc(z_done, 1)

            def dense(i):
                if i < TT:
                    wait(pe, acc_done, STEPS * G - R + i + 1)
                else:
                    wait(pe, y_added, i - TT + 1)
                c = slice(i * P, (i + 1) * P)
                for k in range(KT):
                    three(ps_y[i % TT][:], xT_hi[:, k, c], xT_lo[:, k, c], wbT_hi[:, k, :], wbT_lo[:, k, :], k == 0, False)

            def z_transpose(b):
                wait(pe, zz_done, b + 1)
                wait(pe, late_lo_d, LATE_Z + b - 1)
                for t in range(TT):
                    last = nc.tensor.transpose(ps_tr[b][:, t * P:(t + 1) * P], zz[:, b, t * ER:(t + 1) * ER], ident[:])
                last.then_inc(late_done, 1)

            def lora(i):
                b, c = i // TT, slice(i % TT * P, (i % TT + 1) * P)
                wait(pe, late_lo_d, LATE_Z + b + 1)
                three(ps_y[i % TT][:], zT_hi[:, b, c], zT_lo[:, b, c], lbT_hi, lbT_lo, False, True).then_inc(y_done, 1)

            for t in range(TT - 1):
                out_late(t)
            x1_transpose(0)
            x1_transpose(1)
            out_late(TT - 1)
            for i in range(2, TT):
                x1_transpose(i)
            for i in range(TT):
                z_and_logits(i)
            dense(0)
            x1_transpose(TT)
            x1_transpose(TT + 1)
            dense(1)
            x1_transpose(TT + 2)
            x1_transpose(TT + 3)
            dense(2)
            z_transpose(0)
            for i in range(TT, NT):
                z_and_logits(i)
            for i in range(TT - 1):
                lora(i)
            dense(TT - 1)
            lora(TT - 1)
            dense(TT)
            z_transpose(1)
            dense(TT + 1)
            lora(TT)
            lora(TT + 1)
            for i in range(TT + 2, NT):
                dense(i)
                lora(i)


_INS = ["attn_hidden_states", "attn_Wq", "attn_bq", "attn_Wk", "attn_bk", "attn_Wv", "attn_bv", "attn_Wo", "attn_bo",
        "ffn_W_base", "ffn_b_base", "ffn_lora_A", "ffn_lora_B", "ffn_router_W", "ffn_router_b", "ffn_domain_prior",
        "ffn_active"]


def _shape_constants():
    import numpy as np
    half = D // 2
    f = np.float32
    inv_freq = f(1.0) / np.power(f(10000.0), np.arange(half, dtype=f) / f(half))
    ang = np.arange(S, dtype=f)[None, :] * inv_freq[:, None].astype(f)
    cos, sin = np.cos(ang).astype(f), np.sin(ang).astype(f)
    mask = np.zeros((P, S), f)
    mask[:, S - P:] = np.where(np.arange(P)[None, :] > np.arange(P)[:, None], f(OFF), f(0))
    return {"cos": np.concatenate([cos, cos]), "sin": np.concatenate([-sin, sin]), "ident": np.eye(P, dtype=f),
            "mask": mask, "ids": np.tile(np.arange(E, dtype=f), (P, 1))}


def kernel(**inputs):
    import numpy as np
    import concourse.bacc as bacc
    from concourse.bass_utils import run_bass_kernel_spmd

    nc = bacc.Bacc("TRN2", target_bir_lowering=False, num_devices=1)
    arrays, args = {}, []
    data = [(n, np.ascontiguousarray(inputs["L0_" + n])) for n in _INS] + list(_shape_constants().items())
    for name, a in data:
        arrays[f"in_{name}"] = a
        args.append(nc.dram_tensor(f"in_{name}", a.shape, mybir.dt.from_np(a.dtype), kind="ExternalInput").ap())
    out = nc.dram_tensor("out_0", (B, S, HID), F32, kind="ExternalOutput").ap()
    layer_program(nc, *args, out)
    r = run_bass_kernel_spmd(nc, [arrays], core_ids=[0])
    return r.results[0]["out_0"]
```
